# Optimizing a Trainium2 kernel written in Bass

```python
import numpy as np
import jax
import jax.numpy as jnp

def _softmax(x, axis=-1):
    return jax.nn.softmax(x, axis=axis)

def _gelu(x):
    return jax.nn.gelu(x, approximate=True)

def _silu(x):
    return jax.nn.silu(x)

def _sigmoid(x):
    return jax.nn.sigmoid(x)

def _layernorm(x, axis=-1, eps=1e-05):
    m = jnp.mean(x, axis=axis, keepdims=True)
    v = jnp.var(x, axis=axis, keepdims=True)
    return (x - m) / jnp.sqrt(v + eps)

def _scatter_add(tgt, idx, src, axis=0):
    return tgt.at[idx].add(src)

def _segment_sum(src, seg, n):
    return jax.ops.segment_sum(src, seg, n)
kernel_name = 'mk_decoder_preln_d1_seqx_r4_48fa4e'

def setup_inputs(seed: int=0):
    np.random.seed(seed)
    _w = jnp.asarray

    def _rec_inputs():
        import jax
        import jax.numpy as jnp
        _rk = jax.random.key(seed)
        x = -0.0002928 + 1 * jax.random.normal(jax.random.fold_in(_rk, 1), (32, 256, 256), jnp.float32)
        _lenS = 256 - jax.random.randint(jax.random.fold_in(_rk, 7), (32,), 0, max(1, 256 // 4) + 1, jnp.int32)
        _lenS2 = 256 - jax.random.randint(jax.random.fold_in(_rk, 8), (32,), 0, max(1, 256 // 4) + 1, jnp.int32)
        _ctx_1024P = jax.random.normal(jax.random.fold_in(_rk, 11), (32, 16, 256), jnp.float32)
        _ctx_1024c = jax.random.dirichlet(jax.random.fold_in(_rk, 511), 0.3 * jnp.ones((16,), jnp.float32), (32, 256))
        _ctx_1024t = jnp.einsum('bsk,bkd->bsd', _ctx_1024c, _ctx_1024P)
        _ctx_1024t = _ctx_1024t * jax.lax.rsqrt(jnp.mean(jnp.square(_ctx_1024t)) + 1e-12) * 0.953939
        ctx_1024 = -1.39393e-06 + 0.999914 * (_ctx_1024t + 0.3 * jax.random.normal(jax.random.fold_in(_rk, 611), (32, 256, 256), jnp.float32))
        _validS = jnp.arange(256)[None, :] < _lenS[:, None]
        _validS2 = jnp.arange(256)[None, :] < _lenS2[:, None]
        _causal = jnp.tril(jnp.ones((256, 256), dtype=bool))
        mask_BxS_ik0 = jnp.where(jnp.broadcast_to(_validS[:, :], (32, 256)), 0, 1).astype(jnp.int32)
        return (x, ctx_1024, mask_BxS_ik0)
    x, ctx_1024, mask_BxS_ik0 = _rec_inputs()

    def _L0_attn_setup():
        import jax, jax.numpy as jnp
        import numpy as np
        HEAD_DIM = 64
        N_HEADS = 16
        BASE = 10000.0
        SCALES = (1.0, 4.0, 16.0)

        def _avg_cos_sin(T, head_dim, base, scales):
            pos = jnp.arange(T, dtype=jnp.float32)
            i = jnp.arange(head_dim // 2, dtype=jnp.float32)
            coss, sins = ([], [])
            for s in scales:
                freqs = 1.0 / (base * s) ** (2.0 * i / head_dim)
                ang = pos[:, None] * freqs[None, :]
                coss.append(jnp.cos(ang))
                sins.append(jnp.sin(ang))
            return (jnp.mean(jnp.stack(coss), 0), jnp.mean(jnp.stack(sins), 0))

        def _rope(x, cos, sin):
            xe = x[..., 0::2]
            xo = x[..., 1::2]
            re = xe * cos - xo * sin
            ro = xe * sin + xo * cos
            return jnp.stack([re, ro], axis=-1).reshape(x.shape)
        key = jax.random.key(seed)
        ks = jax.random.split(key, 5)
        B, T, D = (2, 512, 256)
        s = 1.0 / np.sqrt(D)
        return {'x': jax.random.normal(ks[0], (B, T, D), dtype=jnp.float32), 'Wq': jax.random.normal(ks[1], (D, N_HEADS * HEAD_DIM), dtype=jnp.float32) * s, 'Wk': jax.random.normal(ks[2], (D, N_HEADS * HEAD_DIM), dtype=jnp.float32) * s, 'Wv': jax.random.normal(ks[3], (D, N_HEADS * HEAD_DIM), dtype=jnp.float32) * s, 'Wo': jax.random.normal(ks[4], (N_HEADS * HEAD_DIM, D), dtype=jnp.float32) * s}
    _L0_attn_all = _L0_attn_setup()
    _L0_attn_in = {k: v for k, v in _L0_attn_all.items() if k in ('Wq', 'Wk', 'Wv', 'Wo')}
    del _L0_attn_all

    def _L0_xattn_setup():
        import jax, jax.numpy as jnp
        import numpy as np
        HEADS = 16
        DIM_HEAD = 64
        SCALE = DIM_HEAD ** (-0.5)
        MASK_NEG = 1000000.0

        def _split_heads(t):
            b, n, _ = t.shape
            return t.reshape(b, n, HEADS, DIM_HEAD).transpose(0, 2, 1, 3)
        key = jax.random.key(seed)
        ks = jax.random.split(key, 6)
        B, N, M, D = (2, 512, 512, 256)
        inner = HEADS * DIM_HEAD
        x = jax.random.normal(ks[0], (B, N, D), dtype=jnp.float32)
        context = jax.random.normal(ks[1], (B, M, D), dtype=jnp.float32)
        mask = jax.random.randint(ks[2], (B, N), 0, 2, dtype=jnp.int32)
        Wq = jax.random.normal(ks[3], (D, inner), dtype=jnp.float32) * D ** (-0.5)
        Wkv = jax.random.normal(ks[4], (D, 2 * inner), dtype=jnp.float32) * D ** (-0.5)
        Wout = jax.random.normal(ks[5], (inner, D), dtype=jnp.float32) * inner ** (-0.5)
        bout = jnp.zeros((D,), dtype=jnp.float32)
        return {'x': x, 'context': context, 'mask': mask, 'Wq': Wq, 'Wkv': Wkv, 'Wout': Wout, 'bout': bout}
    _L0_xattn_all = _L0_xattn_setup()
    _L0_xattn_in = {k: v for k, v in _L0_xattn_all.items() if k in ('Wq', 'Wkv', 'Wout', 'bout')}
    del _L0_xattn_all

    def _L0_ffn_setup():
        import jax, jax.numpy as jnp
        import numpy as np
        TOP_K = 2
        key = jax.random.key(seed)
        k1, k2, k3 = jax.random.split(key, 3)
        B, S, H, E = (4, 512, 256, 8)
        hidden_states = jax.random.normal(k1, (B, S, H), dtype=jnp.float32)
        Wg = jax.random.normal(k2, (H, E), dtype=jnp.float32) * H ** (-0.5)
        We = jax.random.normal(k3, (E, H, H), dtype=jnp.float32) * H ** (-0.5)
        be = jnp.zeros((E, H), dtype=jnp.float32)
        return {'hidden_states': hidden_states, 'Wg': Wg, 'We': We, 'be': be}
    _L0_ffn_all = _L0_ffn_setup()
    _L0_ffn_in = {k: v for k, v in _L0_ffn_all.items() if k in ('Wg', 'We', 'be')}
    del _L0_ffn_all
    return {'x': x, 'ctx_1024': ctx_1024, 'mask_BxS_ik0': mask_BxS_ik0, 'L0_attn_Wq': _L0_attn_in['Wq'], 'L0_attn_Wk': _L0_attn_in['Wk'], 'L0_attn_Wv': _L0_attn_in['Wv'], 'L0_attn_Wo': _L0_attn_in['Wo'], 'L0_xattn_Wq': _L0_xattn_in['Wq'], 'L0_xattn_Wkv': _L0_xattn_in['Wkv'], 'L0_xattn_Wout': _L0_xattn_in['Wout'], 'L0_xattn_bout': _L0_xattn_in['bout'], 'L0_ffn_Wg': _L0_ffn_in['Wg'], 'L0_ffn_We': _L0_ffn_in['We'], 'L0_ffn_be': _L0_ffn_in['be']}

def reference(x, ctx_1024, mask_BxS_ik0, L0_attn_Wq, L0_attn_Wk, L0_attn_Wv, L0_attn_Wo, L0_xattn_Wq, L0_xattn_Wkv, L0_xattn_Wout, L0_xattn_bout, L0_ffn_Wg, L0_ffn_We, L0_ffn_be):
    import jax
    import jax.numpy as jnp

    def _L0_attn_ref(x, Wq, Wk, Wv, Wo):
        import jax, jax.numpy as jnp
        import numpy as np
        HEAD_DIM = 64
        N_HEADS = 16
        BASE = 10000.0
        SCALES = (1.0, 4.0, 16.0)

        def _avg_cos_sin(T, head_dim, base, scales):
            pos = jnp.arange(T, dtype=jnp.float32)
            i = jnp.arange(head_dim // 2, dtype=jnp.float32)
            coss, sins = ([], [])
            for s in scales:
                freqs = 1.0 / (base * s) ** (2.0 * i / head_dim)
                ang = pos[:, None] * freqs[None, :]
                coss.append(jnp.cos(ang))
                sins.append(jnp.sin(ang))
            return (jnp.mean(jnp.stack(coss), 0), jnp.mean(jnp.stack(sins), 0))

        def _rope(x, cos, sin):
            xe = x[..., 0::2]
            xo = x[..., 1::2]
            re = xe * cos - xo * sin
            ro = xe * sin + xo * cos
            return jnp.stack([re, ro], axis=-1).reshape(x.shape)
        B, T, D = x.shape
        H, hd = (N_HEADS, HEAD_DIM)
        q = (x @ Wq).reshape(B, T, H, hd).transpose(0, 2, 1, 3)
        k = (x @ Wk).reshape(B, T, H, hd).transpose(0, 2, 1, 3)
        v = (x @ Wv).reshape(B, T, H, hd).transpose(0, 2, 1, 3)
        cos, sin = _avg_cos_sin(T, hd, BASE, SCALES)
        q = _rope(q, cos, sin)
        k = _rope(k, cos, sin)
        scale = 1.0 / np.sqrt(hd).astype(np.float32)
        attn = jax.nn.softmax(jnp.einsum('bhqd,bhkd->bhqk', q, k) * scale, axis=-1)
        out = jnp.einsum('bhqk,bhkd->bhqd', attn, v)
        out = out.transpose(0, 2, 1, 3).reshape(B, T, H * hd)
        return out @ Wo

    def _L0_xattn_ref(x, context, mask, Wq, Wkv, Wout, bout):
        import jax, jax.numpy as jnp
        import numpy as np
        HEADS = 16
        DIM_HEAD = 64
        SCALE = DIM_HEAD ** (-0.5)
        MASK_NEG = 1000000.0

        def _split_heads(t):
            b, n, _ = t.shape
            return t.reshape(b, n, HEADS, DIM_HEAD).transpose(0, 2, 1, 3)
        kv = context @ Wkv
        k, v = jnp.split(kv, 2, axis=-1)
        q = x @ Wq
        q, k, v = (_split_heads(q), _split_heads(k), _split_heads(v))
        dots = jnp.einsum('bhnd,bhmd->bhnm', q, k) * SCALE
        dots = dots - (1.0 - mask.astype(jnp.float32))[:, None, :, None] * MASK_NEG
        attn = jax.nn.softmax(dots, axis=-1)
        out = jnp.einsum('bhnm,bhmd->bhnd', attn, v)
        b, h, n, d = out.shape
        out = out.transpose(0, 2, 1, 3).reshape(b, n, h * d)
        return out @ Wout + bout

    def _L0_ffn_ref(hidden_states, Wg, We, be):
        import jax, jax.numpy as jnp
        import numpy as np
        TOP_K = 2
        B, S, H = hidden_states.shape
        T = B * S
        x = hidden_states.reshape(T, H)
        probs = jax.nn.softmax(x @ Wg, axis=-1)
        top_vals, top_idx = jax.lax.top_k(probs, TOP_K)
        gates = top_vals / jnp.sum(top_vals, axis=-1, keepdims=True)
        expert_out = jnp.einsum('th,ehd->etd', x, We) + be[:, None, :]
        tok = jnp.arange(T)[:, None]
        sel = expert_out[top_idx, tok, :]
        out = jnp.sum(gates[..., None] * sel, axis=1)
        return out.reshape(B, S, H)
    x = x + _L0_attn_ref(_layernorm(x, axis=-1), L0_attn_Wq, L0_attn_Wk, L0_attn_Wv, L0_attn_Wo)
    x = x + _L0_xattn_ref(_layernorm(x, axis=-1), ctx_1024, mask_BxS_ik0, L0_xattn_Wq, L0_xattn_Wkv, L0_xattn_Wout, L0_xattn_bout)
    x = x + _L0_ffn_ref(_layernorm(x, axis=-1), L0_ffn_Wg, L0_ffn_We, L0_ffn_be)
    return x

_drawn_inputs = setup_inputs


def setup_inputs(seed=0):
    import zlib

    import numpy as np

    out = dict(_drawn_inputs(seed))
    spreads = {'L0_xattn_bout': (0.0, 0.1), 'L0_ffn_be': (0.0, 0.1)}
    factors = {}
    for name, (base, spread) in spreads.items():
        noise = np.random.default_rng([zlib.crc32(name.encode()), seed]).standard_normal(out[name].shape)
        drawn = base * np.exp(spread * noise) if base else spread * noise
        out[name] = jnp.asarray(drawn.astype(out[name].dtype))
    for name, factor in factors.items():
        out[name] = (out[name] * factor).astype(out[name].dtype)
    return out
```

```python
from contextlib import ExitStack

import numpy as np
import concourse.bass as bass
from concourse import mybir

F32 = mybir.dt.float32
F32R = mybir.dt.float32r
I32 = mybir.dt.int32
U32 = mybir.dt.uint32
ALU = mybir.AluOpType
ACT = mybir.ActivationFunctionType
AX = mybir.AxisListType

B, T, D = 32, 256, 256
H, HD = 16, 64
E = 8
P = 128
NT = T // P
NC = D // P
HG = 4
GW = HG * HD
NG = H // HG
NH = 2 * H
HALF = HD // 2
SCALE = HD ** -0.5
MASK_NEG = 1000000.0
EPS = 1e-5

SLOTS = 36
DRAIN = (16, 20)
P_BUFS = 3
GATE_STEPS = 8
STATS = 4


def head_in(s):
    off, s = divmod(s, SLOTS)
    if DRAIN[0] <= s < DRAIN[1]:
        return None
    return off, (s if s < DRAIN[0] else s - (DRAIN[1] - DRAIN[0])), s


def meets_values(s):
    if s % SLOTS == DRAIN[0] + 1:
        return head_in(s - 3)
    if s % 2 or s % SLOTS == DRAIN[0] + 2:
        return None
    return head_in(s - 4)


def projects(s):
    if s % SLOTS == DRAIN[0] + 2:
        return head_in(s - 4)
    pair = meets_values(s - 1)
    return pair if pair and pair[1] % HG == 2 and s % SLOTS != DRAIN[0] + 2 else None


UNITS = {s: [] for s in range(SLOTS)}
for _s, _u in (
        (0, ("QT", 1, 0)), (0, ("KP", 1, 0)), (2, ("KT", 1, 0)), (2, ("V", 1, 0)),
        (3, ("QP", 2, 0)), (4, ("QT", 2, 0)), (4, ("KP", 2, 0)), (6, ("KT", 2, 0)), (6, ("V", 2, 0)),
        (7, ("QP", 3, 0)), (8, ("QT", 3, 0)), (8, ("KP", 3, 0)), (10, ("KT", 3, 0)), (10, ("V", 3, 0)),
        (5, ("L3", 0, -1)), (7, ("LG", 0, -1)), (9, ("GT", 0, -1)), (11, ("BI", 0, -1)),
        (12, ("EX", 0, -1)), (13, ("EX", 1, -1)), (14, ("EX", 2, -1)), (15, ("EX", 3, -1)),
        (17, ("EX", 4, -1)), (18, ("EX", 5, -1)), (18, ("EX", 6, -1)), (18, ("EX", 7, -1)),
        (11, ("CT", 0, 0)), (12, ("KT", 4, 0)), (14, ("V", 4, 0)), (16, ("KT", 5, 0)),
        (19, ("L2", 0, 0)), (19, ("V", 5, 0)), (19, ("QT", 4, 0)), (19, ("QT", 5, 0)),
        (24, ("KT", 6, 0)), (25, ("QT", 6, 0)), (26, ("V", 6, 0)),
        (28, ("KT", 7, 0)), (29, ("QT", 7, 0)), (30, ("V", 7, 0)),
        (29, ("L1", 0, 1)), (31, ("QP", 0, 1)), (32, ("QT", 0, 1)), (32, ("KP", 0, 1)),
        (34, ("KT", 0, 1)), (34, ("V", 0, 1)), (35, ("QP", 1, 1))):
    UNITS[_s] += [_u]
FLAT = [u for s in range(SLOTS) for u in UNITS[s]]


def layer(nc, x_d, ctx_d, mask_d, sq_d, sk_d, sv_d, so_d, cq_d, ckv_d, co_d, bout_d, wg_d, we_d,
          be_d, cos_d, sin_d, iota_d, out_d):
    ctx = ExitStack()
    with ctx:
        def sb(name, shape, dt=F32):
            return ctx.enter_context(nc.sbuf_tensor(name, shape, dt))

        class Signal:

            def __init__(self, name, per, step=1):
                self.sem = ctx.enter_context(nc.semaphore(name))
                self.per, self.step = per, step

            def at(self, b, off, k):
                value = b * (self.per * self.step) + (off * self.per + k) * self.step
                return max(value, 0) if isinstance(b, int) else value

        w_hi = sb("w_hi", [P, 8, NC * H * HD], F32R)
        w_lo = sb("w_lo", [P, 8, NC * H * HD], F32R)
        we_hi = sb("we_hi", [P, NC, E * D], F32R)
        we_lo = sb("we_lo", [P, NC, E * D], F32R)
        wg_f = sb("wg_f", [P, NC, E])
        wg_hi = sb("wg_hi", [P, NC, E], F32R)
        wg_lo = sb("wg_lo", [P, NC, E], F32R)
        be_sb = sb("be_sb", [E, D])[:]
        gatesT = sb("gatesT", [E, T])[:]
        bout_sb = sb("bout_sb", [P, D])
        cos_sb = sb("cos_sb", [P, NT, HALF])
        sin_sb = sb("sin_sb", [P, NT, HALF])
        iota_sb = sb("iota_sb", [P, E])
        ident = sb("ident", [P, P])
        neg_half = sb("neg_half", [P, NT])

        x_in = sb("x_in", [P, NT, D])
        x1 = sb("x1", [P, NT, D])
        xn = sb("xn", [P, NT, D])
        ctx_in = sb("ctx_in", [P, NT, D])
        xs_hi, xs_lo = sb("xs_hi", [P, NC, T], F32R), sb("xs_lo", [P, NC, T], F32R)
        xc_hi, xc_lo = sb("xc_hi", [P, NC, T], F32R), sb("xc_lo", [P, NC, T], F32R)
        ct_hi, ct_lo = sb("ct_hi", [P, NC, T], F32R), sb("ct_lo", [P, NC, T], F32R)
        rope_a = sb("rope_a", [P, NT, GW])
        rope_b = sb("rope_b", [P, NT, GW])
        qT_hi, qT_lo = sb("qT_hi", [P, 2, 2, T], F32R), sb("qT_lo", [P, 2, 2, T], F32R)
        kT_hi, kT_lo = sb("kT_hi", [P, 2, 2, T], F32R), sb("kT_lo", [P, 2, 2, T], F32R)
        v_sb = sb("v_sb", [P, 2, NT, GW])
        probs = sb("probs", [P, P_BUFS, NT, T])
        pT = sb("pT", [P, 2, NT, T])
        oT_hi, oT_lo = sb("oT_hi", [P, 2, T], F32R), sb("oT_lo", [P, 2, T], F32R)

        neg_max = sb("neg_max", [P, STATS, NT])
        row_max = sb("row_max", [P, STATS, NT])
        row_sum = sb("row_sum", [P, STATS, NT])
        inv_sum = sb("inv_sum", [P, STATS, NT])
        mask_i = sb("mask_i", [P, NT], I32)
        mask_add = sb("mask_add", [P, NT])
        bn = sb("bn", [P, 3, NT, 6])
        mean_var = sb("mean_var", [P, 3, NT, 2])
        var_eps = sb("var_eps", [P, 3, NT])
        rstd = sb("rstd", [P, 3, NT])
        g_nmax = sb("g_nmax", [P, NT])
        g_exp = sb("g_exp", [P, NT, E])
        g_sum = sb("g_sum", [P, NT])
        g_inv = sb("g_inv", [P, NT])
        g_prob = sb("g_prob", [P, NT, E])
        g_top = sb("g_top", [P, NT, 8])
        g_idx = sb("g_idx", [P, NT, 8], U32)
        g_idf = sb("g_idf", [P, NT, 8])
        g_two = sb("g_two", [P, NT, 1])
        g_rtwo = sb("g_rtwo", [P, NT, 1])
        g_val = sb("g_val", [P, NT, 2])
        g_first = sb("g_first", [P, NT, E])
        g_second = sb("g_second", [P, NT, E])
        gates = sb("gates", [P, NT, E])
        waiter = sb("waiter", [P, 1])

        def bank(name):
            return ctx.enter_context(nc.psum_tensor(name, [P, 512], F32))

        score_ps = [bank(f"score_ps{i}") for i in range(2)]
        pT_ps = [bank(f"pT_ps{i}") for i in range(2)]
        unit_ps = [bank(f"unit_ps{i}") for i in range(2)]
        oT_ps = bank("oT_ps")
        wo_ps = bank("wo_ps")

        stage_in = [ctx.enter_context(nc.semaphore(f"stage_in{i}")) for i in range(P_BUFS + 2)]
        small_in = ctx.enter_context(nc.semaphore("small_in"))
        stage_hi = ctx.enter_context(nc.semaphore("stage_hi"))
        stage_done = ctx.enter_context(nc.semaphore("stage_done"))
        wg_split = ctx.enter_context(nc.semaphore("wg_split"))
        consts = ctx.enter_context(nc.semaphore("consts"))
        x_loaded = Signal("x_loaded", 1, 16)
        ctx_loaded = Signal("ctx_loaded", 1, 16)
        mask_loaded = Signal("mask_loaded", 1, 16)
        stored = Signal("stored", 1, 16)
        scored = Signal("scored", NH)
        probs_turned = Signal("probs_turned", NH)
        pv_done = Signal("pv_done", NH // 2)
        wo_done = Signal("wo_done", 2 * NG)
        qk_projected = Signal("qk_projected", 2 * NG)
        v_projected = Signal("v_projected", 2 * NG)
        q_turned = Signal("q_turned", 2 * NG)
        k_turned = Signal("k_turned", 2 * NG)
        ctx_turned = Signal("ctx_turned", 1)
        xs_turned = Signal("xs_turned", 1)
        xc_turned = Signal("xc_turned", 2)
        logits_done = Signal("logits_done", 1)
        gates_turned = Signal("gates_turned", 1)
        bias_done = Signal("bias_done", 1)
        expert_done = Signal("expert_done", E)
        exp_done = Signal("exp_done", NH)
        pT_ready = Signal("pT_ready", NH)
        q_hi_ready = Signal("q_hi_ready", 2 * NG)
        k_hi_ready = Signal("k_hi_ready", 2 * NG)
        ctx_hi_ready = Signal("ctx_hi_ready", 1)
        xs_hi_ready = Signal("xs_hi_ready", 1)
        xc_hi_ready = Signal("xc_hi_ready", 2)
        oT_hi_ready = Signal("oT_hi_ready", 2 * NG)
        v_ready = Signal("v_ready", 2 * NG)
        gate_exp = Signal("gate_exp", 1)
        max_found = Signal("max_found", H)
        max_ready = Signal("max_ready", NH)
        inv_ready = Signal("inv_ready", NH)
        rope_split = Signal("rope_split", 2 * NG)
        q_ready = Signal("q_ready", 2 * NG)
        k_ready = Signal("k_ready", 2 * NG)
        ctx_ready = Signal("ctx_ready", 1)
        xs_ready = Signal("xs_ready", 1)
        xc_ready = Signal("xc_ready", 2)
        oT_ready = Signal("oT_ready", 2 * NG)
        resid_done = [Signal(f"resid_done{i}", 1) for i in range(2)]
        x_moved = Signal("x_moved", 1)
        mask_ready = Signal("mask_ready", 1)
        ln_step = [Signal(f"ln_step{i}", 3) for i in range(3)]
        ln_out = [Signal(f"ln_out{i}", 1) for i in range(3)]
        gate_max = Signal("gate_max", 1)
        gate_step = Signal("gate_step", GATE_STEPS)
        gatesT_ready = Signal("gatesT_ready", 1)
        bias_added = Signal("bias_added", 1)
        expert_added = Signal("expert_added", 2 * E)
        probs_ready = Signal("probs_ready", NH)
        roped = Signal("roped", 2 * NG)
        rope_step = Signal("rope_step", 2 * NG)
        rstd_ready = [Signal(f"rstd_ready{i}", 1) for i in range(3)]

        def exists(b, off):
            return not isinstance(b, int) or 0 <= b + off < B

        def read_signal(kind, g):
            return {"QP": (rope_split, 2 * g + 1), "KP": (rope_split, 2 * g + 2), "V": (v_ready, g + 1),
                    "QT": (q_ready, g + 1), "KT": (k_ready, g + 1), "CT": (ctx_ready, 1),
                    "L1": (xs_ready, 1), "L2": (xc_ready, 1), "L3": (xc_ready, 2), "LG": (gate_exp, 1),
                    "GT": (gatesT_ready, 1), "BI": (bias_added, 1), "EX": (expert_added, 2 * g + 2)}[kind]

        def bank_before(b, at):
            prev, back = at - 1, 0
            while back > -2:
                if prev < 0:
                    prev, back = len(FLAT) - 1, back - 1
                kind, g, off = FLAT[prev]
                if prev % 2 == at % 2 and exists(b, off + back):
                    signal, k = read_signal(kind, g)
                    return signal, off + back, k
                prev -= 1
            return stored, -1, 0

        def unit_bank(s, n):
            return sum(len(UNITS[i]) for i in range(s)) + n

        def flat(ap):
            return ap.rearrange("p a n -> p (a n)")

        def pieces(hi, lo):
            return ((lo[0], hi[1]), (hi[0], lo[1]), (hi[0], hi[1]))

        stages = [probs[:, i, :, :].rearrange("p a n -> p (a n)") for i in range(P_BUFS)] + \
                 [pT[:, i, :, :].rearrange("p a n -> p (a n)") for i in range(2)]

        def stage_list():
            out = []
            for m, (w, c0) in enumerate(((sq_d, 0), (sk_d, 0), (sv_d, 0), (so_d, None), (cq_d, 0),
                                         (ckv_d, 0), (ckv_d, H * HD), (co_d, None))):
                for j in range(4):
                    if c0 is None:
                        src = w[2 * j * P:(2 * j + 2) * P, :].rearrange("(c p) n -> p c n", p=P)
                    else:
                        c, n = divmod(j, 2)
                        src = w[c * P:(c + 1) * P, c0 + n * 512:c0 + (n + 1) * 512]
                    out.append((src, w_hi[:, m, j * 512:(j + 1) * 512], w_lo[:, m, j * 512:(j + 1) * 512]))
            for c in range(NC):
                for j in range(E // 2):
                    src = we_d[2 * j:2 * j + 2, c * P:(c + 1) * P, :].rearrange("e p n -> p e n")
                    out.append((src, we_hi[:, c, j * 512:(j + 1) * 512], we_lo[:, c, j * 512:(j + 1) * 512]))
            return out

        STAGES = stage_list()
        def bodies(engine, body):
            body(-1)
            body(0)
            with engine.Fori(1, B - 1) as b:
                body(b)
            body(B - 1)
            body(B)

        block = ctx.enter_context(nc.Block())

        @block.sync
        def _(sp):
            for j, (src, _, _) in enumerate(STAGES):
                slot = j % len(stages)
                if j >= len(stages):
                    sp.wait_ge(stage_done, j - len(stages) + 1)
                dst = stages[slot]
                if len(src.shape) == 3:
                    dst = dst.rearrange("p (c n) -> p c n", c=2)
                sp.dma_start(dst, src).then_inc(stage_in[slot], 16)

            def body(b):
                if exists(b, 1):
                    sp.wait_ge(ctx_turned.sem, ctx_turned.at(b, 0, 1))
                    sp.dma_start(ctx_in[:], ctx_d[b + 1].rearrange("(t p) d -> p t d", p=P)) \
                        .then_inc(ctx_loaded.sem, 16)
                    sp.wait_ge(mask_ready.sem, mask_ready.at(b, 0, 1))
                    sp.dma_start(mask_i[:], mask_d[b + 1]).then_inc(mask_loaded.sem, 16)
                if exists(b, -1):
                    sp.wait_ge(expert_added.sem, expert_added.at(b, -1, 2 * E))
                    sp.dma_start(out_d[b - 1].rearrange("(t p) d -> p t d", p=P), x1[:]).then_inc(stored.sem, 16)
                if exists(b, 1):
                    sp.wait_ge(x_moved.sem, x_moved.at(b, 0, 1))
                    sp.dma_start(x_in[:], x_d[b + 1].rearrange("(t p) d -> p t d", p=P)).then_inc(x_loaded.sem, 16)

            bodies(sp, body)
            sp.wait_ge(stored.sem, 16 * B)

        @block.tensor
        def _(pe):
            pe.wait_ge(stage_done, len(STAGES))
            pe.wait_ge(wg_split, 2)
            pe.wait_ge(consts, 3)

            def token_major(ps, src_hi, src_lo, m, g):
                for t in range(NT):
                    n = 0
                    for c in range(NC):
                        for a, w in pieces((src_hi, w_hi), (src_lo, w_lo)):
                            cols = c * H * HD + g * GW
                            last = nc.tensor.matmul(ps[:, t * GW:(t + 1) * GW], a[:, c, t * P:(t + 1) * P],
                                                    w[:, m, cols:cols + GW], start=n == 0, stop=n == 3 * NC - 1)
                            n += 1
                return last

            def dim_major(ps, src_hi, src_lo, m, g):
                for j in range(2):
                    n = 0
                    for c in range(NC):
                        for w, a in pieces((w_hi, src_hi), (w_lo, src_lo)):
                            cols = c * H * HD + g * GW + j * P
                            last = nc.tensor.matmul(ps[:, j * T:(j + 1) * T], w[:, m, cols:cols + P],
                                                    a[:, c, :], start=n == 0, stop=n == 3 * NC - 1)
                            n += 1
                return last

            def tile_product(ps, t, w_hi_, w_lo_, c0, width):
                i = 0
                for c in range(NC):
                    for a, w in pieces((xc_hi, w_hi_), (xc_lo, w_lo_)):
                        last = nc.tensor.matmul(ps, a[:, c, t * P:(t + 1) * P], w[:, c, c0:c0 + width],
                                                start=i == 0, stop=i == 3 * NC - 1)
                        i += 1
                return last

            def turn(ps, src):
                for c in range(2):
                    for t in range(NT):
                        last = nc.tensor.transpose(ps[:, c * T + t * P:c * T + (t + 1) * P],
                                                   src[:, t, c * P:(c + 1) * P], ident[:])
                return last

            def unit(b, s, n, kind, g, off):
                at = unit_bank(s, n)
                ps = unit_ps[at % 2]
                before, boff, k = bank_before(b, at)
                pe.wait_ge(before.sem, before.at(b, boff, k))
                if kind in ("QP", "KP"):
                    pe.wait_ge(xs_ready.sem, xs_ready.at(b, off, 1))
                    token_major(ps, xs_hi, xs_lo, 0 if kind == "QP" else 1, g).then_inc(qk_projected.sem, 1)
                elif kind == "V" and g < NG:
                    pe.wait_ge(xs_ready.sem, xs_ready.at(b, off, 1))
                    token_major(ps, xs_hi, xs_lo, 2, g).then_inc(v_projected.sem, 1)
                elif kind == "V":
                    pe.wait_ge(ctx_ready.sem, ctx_ready.at(b, off, 1))
                    token_major(ps, ct_hi, ct_lo, 6, g - NG).then_inc(v_projected.sem, 1)
                elif kind == "QT" and g < NG:
                    pe.wait_ge(roped.sem, roped.at(b, off, 2 * g + 1))
                    turn(ps, rope_a).then_inc(q_turned.sem, 1)
                elif kind == "KT" and g < NG:
                    pe.wait_ge(roped.sem, roped.at(b, off, 2 * g + 2))
                    turn(ps, rope_a).then_inc(k_turned.sem, 1)
                elif kind == "QT":
                    pe.wait_ge(xc_ready.sem, xc_ready.at(b, off, 1))
                    dim_major(ps, xc_hi, xc_lo, 4, g - NG).then_inc(q_turned.sem, 1)
                elif kind == "KT":
                    pe.wait_ge(ctx_ready.sem, ctx_ready.at(b, off, 1))
                    dim_major(ps, ct_hi, ct_lo, 5, g - NG).then_inc(k_turned.sem, 1)
                elif kind == "CT":
                    pe.wait_ge(ctx_loaded.sem, ctx_loaded.at(b, off, 1))
                    turn(ps, ctx_in).then_inc(ctx_turned.sem, 1)
                elif kind == "L1":
                    pe.wait_ge(ln_out[0].sem, ln_out[0].at(b, off, 1))
                    turn(ps, xn).then_inc(xs_turned.sem, 1)
                elif kind in ("L2", "L3"):
                    i = 1 if kind == "L2" else 2
                    pe.wait_ge(ln_out[i].sem, ln_out[i].at(b, off, 1))
                    turn(ps, xn).then_inc(xc_turned.sem, 1)
                elif kind == "LG":
                    pe.wait_ge(xc_ready.sem, xc_ready.at(b, off, 2))
                    for t in range(NT):
                        last = tile_product(ps[:, t * E:(t + 1) * E], t, wg_hi, wg_lo, 0, E)
                    last.then_inc(logits_done.sem, 1)
                elif kind == "GT":
                    pe.wait_ge(gate_step.sem, gate_step.at(b, off, GATE_STEPS))
                    for t in range(NT):
                        last = nc.tensor.transpose(ps[0:E, t * P:(t + 1) * P], gates[:, t, :], ident[:])
                    last.then_inc(gates_turned.sem, 1)
                elif kind == "BI":
                    pe.wait_ge(gatesT_ready.sem, gatesT_ready.at(b, off, 1))
                    for t in range(NT):
                        last = nc.tensor.matmul(ps[:, t * D:(t + 1) * D], gatesT[:, t * P:(t + 1) * P],
                                                be_sb, start=True, stop=True)
                    last.then_inc(bias_done.sem, 1)
                else:
                    j, t = divmod(g, NT)
                    tile_product(ps[:], t, we_hi, we_lo, 2 * j * D, 2 * D).then_inc(expert_done.sem, 1)

            def scores(b, s, h):
                g, hl = divmod(h, HG)
                back = next(head_in(s - i) for i in (2, 4, 6, 8) if head_in(s - i))
                read = exp_done if back[1] < H else max_ready
                pe.wait_ge(read.sem, read.at(b, back[0], back[1] + 1))
                if hl == 0:
                    pe.wait_ge(q_ready.sem, q_ready.at(b, 0, g + 1))
                    pe.wait_ge(k_ready.sem, k_ready.at(b, 0, g + 1))
                r, c = HD * (hl % 2), hl // 2
                for t in range(NT):
                    for i, (q, k) in enumerate(pieces((qT_hi, kT_hi), (qT_lo, kT_lo))):
                        last = nc.tensor.matmul(score_ps[s % 2][:, t * T:(t + 1) * T],
                                                q[r:r + HD, g % 2, c, t * P:(t + 1) * P],
                                                k[r:r + HD, g % 2, c, :], start=i == 0, stop=i == 2)
                last.then_inc(scored.sem, 1)

            def turn_probs(b, s):
                off, h, hs = head_in(s - 2)
                if not exists(b, off):
                    return
                back = next(head_in(s - 2 - i) for i in (2, 4, 6, 8) if head_in(s - 2 - i))
                pe.wait_ge(pT_ready.sem, pT_ready.at(b, back[0], back[1] + 1))
                pe.wait_ge(probs_ready.sem, probs_ready.at(b, off, h + 1))
                for k in range(NT):
                    for t in range(NT):
                        last = nc.tensor.transpose(pT_ps[s % 2][:, k * T + t * P:k * T + (t + 1) * P],
                                                   probs[:, hs % P_BUFS, t, k * P:(k + 1) * P], ident[:])
                last.then_inc(probs_turned.sem, 1)

            def values(b, s):
                off, h, hs = meets_values(s)
                if not exists(b, off):
                    return
                g, hl = divmod(h, HG)
                pe.wait_ge(pT_ready.sem, pT_ready.at(b, off, h + 2))
                if hl == 0:
                    pe.wait_ge(v_ready.sem, v_ready.at(b, off, g + 1))
                    pe.wait_ge(oT_ready.sem, oT_ready.at(b, off, g))
                for k in range(NT):
                    for i in range(2):
                        slot = (hs + i) % 2
                        last = nc.tensor.matmul(oT_ps[i * HD:(i + 1) * HD, (hl // 2) * T:(hl // 2 + 1) * T],
                                                v_sb[:, g % 2, k, (hl + i) * HD:(hl + i + 1) * HD],
                                                pT[:, slot, k, :], start=k == 0, stop=k == NT - 1,
                                                skip_group_check=True)
                last.then_inc(pv_done.sem, 1)

            def project(b, s):
                off, h, _ = projects(s)
                if not exists(b, off):
                    return
                g = h // HG
                if g == 0:
                    pe.wait_ge(resid_done[1].sem, resid_done[1].at(b, off - 1, 1))
                if g == NG:
                    pe.wait_ge(resid_done[0].sem, resid_done[0].at(b, off, 1))
                pe.wait_ge(oT_ready.sem, oT_ready.at(b, off, g + 1))
                m = 3 if g < NG else 7
                gg = g % NG
                for t in range(NT):
                    for c in range(2):
                        for i, (o, w) in enumerate(pieces((oT_hi, w_hi), (oT_lo, w_lo))):
                            cols = (2 * gg + c) * D
                            last = nc.tensor.matmul(wo_ps[:, t * D:(t + 1) * D], o[:, c, t * P:(t + 1) * P],
                                                    w[:, m, cols:cols + D],
                                                    start=gg == 0 and t == 0 and c == 0 and i == 0,
                                                    stop=gg == NG - 1 and c == 1 and i == 2,
                                                    skip_group_check=True)
                last.then_inc(wo_done.sem, 1)

            def body(b):
                for s in range(SLOTS):
                    if head_in(s) and exists(b, 0):
                        scores(b, s, head_in(s)[1])
                    if meets_values(s) and s != DRAIN[0] + 1:
                        values(b, s)
                    if head_in(s - 2):
                        turn_probs(b, s)
                    if s == DRAIN[0] + 2:
                        project(b, s)
                    for n, (kind, g, off) in enumerate(UNITS[s]):
                        if exists(b, off):
                            unit(b, s, n, kind, g, off)
                    if s == DRAIN[0] + 1:
                        values(b, s)
                    if projects(s) and s != DRAIN[0] + 2:
                        project(b, s)

            bodies(pe, body)

        @block.scalar
        def _(act):
            for dst, src in ((wg_f[:], wg_d.rearrange("(c p) e -> p c e", p=P)), (be_sb, be_d),
                             (bout_sb[:], bout_d.partition_broadcast(P)), (iota_sb[:], iota_d),
                             (cos_sb[:], cos_d), (sin_sb[:], sin_d)):
                act.dma_start(dst, src).then_inc(small_in, 16)
            for j, (_, hi, _) in enumerate(STAGES):
                act.wait_ge(stage_in[j % len(stages)], 16 * (j // len(stages) + 1))
                nc.scalar.activation(hi, stages[j % len(stages)], ACT.Copy).then_inc(stage_hi, 1)
            act.wait_ge(small_in, 96)
            nc.scalar.activation(wg_hi[:], wg_f[:], ACT.Copy).then_inc(wg_split, 1)
            act.wait_ge(stage_done, len(STAGES))

            def unit(b, ps, kind, g, off):
                if kind == "V":
                    act.wait_ge(v_projected.sem, v_projected.at(b, off, g + 1))
                    nc.scalar.activation(flat(v_sb[:, g % 2, :, :]), ps, ACT.Copy).then_inc(v_ready.sem, 1)
                elif kind == "QT":
                    act.wait_ge(q_turned.sem, q_turned.at(b, off, g + 1))
                    nc.scalar.activation(flat(qT_hi[:, g % 2, :, :]), ps, ACT.Copy,
                                         scale=SCALE).then_inc(q_hi_ready.sem, 1)
                elif kind == "KT":
                    act.wait_ge(k_turned.sem, k_turned.at(b, off, g + 1))
                    nc.scalar.activation(flat(kT_hi[:, g % 2, :, :]), ps, ACT.Copy).then_inc(k_hi_ready.sem, 1)
                elif kind == "CT":
                    act.wait_ge(ctx_turned.sem, ctx_turned.at(b, off, 1))
                    nc.scalar.activation(flat(ct_hi[:]), ps, ACT.Copy).then_inc(ctx_hi_ready.sem, 1)
                elif kind == "L1":
                    act.wait_ge(xs_turned.sem, xs_turned.at(b, off, 1))
                    nc.scalar.activation(flat(xs_hi[:]), ps, ACT.Copy).then_inc(xs_hi_ready.sem, 1)
                elif kind in ("L2", "L3"):
                    act.wait_ge(xc_turned.sem, xc_turned.at(b, off, 1 if kind == "L2" else 2))
                    nc.scalar.activation(flat(xc_hi[:]), ps, ACT.Copy).then_inc(xc_hi_ready.sem, 1)
                elif kind == "LG":
                    act.wait_ge(gate_max.sem, gate_max.at(b, off, 1))
                    for t in range(NT):
                        last = nc.scalar.activation(g_exp[:, t, :], ps[:, t * E:(t + 1) * E], ACT.Exp,
                                                    bias=g_nmax[:, t:t + 1], accum_out=g_sum[:, t:t + 1])
                    last.then_inc(gate_exp.sem, 1)

            def body(b):
                for s in range(SLOTS):
                    turned = head_in(s - 2)
                    if turned and exists(b, turned[0]):
                        off, h, _ = turned
                        back = next(head_in(s - 2 - i) for i in (2, 4, 6, 8) if head_in(s - 2 - i))
                        act.wait_ge(pv_done.sem, pv_done.at(b, back[0], back[1] // 2 + 1))
                        act.wait_ge(probs_turned.sem, probs_turned.at(b, off, h + 1))
                        nc.scalar.activation(
                            flat(pT[:, s % 2, :, :]), pT_ps[s % 2][:], ACT.Copy).then_inc(pT_ready.sem, 1)
                    here = head_in(s)
                    if here and exists(b, 0):
                        h = here[1]
                        back = next(head_in(s - i) for i in (3, 6, 9) if head_in(s - i))
                        act.wait_ge(probs_turned.sem, probs_turned.at(b, back[0], back[1] + 1))
                        act.wait_ge(max_ready.sem, max_ready.at(b, 0, h + 1))
                        for t in range(NT):
                            dst = probs[:, s % P_BUFS, t, :]
                            src = score_ps[s % 2][:, t * T:(t + 1) * T] if h < H else dst
                            last = nc.scalar.activation(dst, src, ACT.Exp, bias=neg_max[:, h % STATS, t:t + 1],
                                                        accum_out=row_sum[:, h % STATS, t:t + 1])
                        last.then_inc(exp_done.sem, 1)
                    for n, (kind, g, off) in enumerate(UNITS[s]):
                        if exists(b, off):
                            unit(b, unit_ps[unit_bank(s, n) % 2][:], kind, g, off)
                    pair = meets_values(s)
                    if pair and pair[1] % HG == 2 and exists(b, pair[0]):
                        off, h, _ = pair
                        act.wait_ge(pv_done.sem, pv_done.at(b, off, h // 2 + 1))
                        nc.scalar.activation(flat(oT_hi[:]), oT_ps[:],
                                                            ACT.Copy).then_inc(oT_hi_ready.sem, 1)

            bodies(act, body)

        @block.vector
        def _(dve):
            for j, (_, hi, lo) in enumerate(STAGES):
                dve.wait_ge(stage_hi, j + 1)
                nc.vector.tensor_tensor(lo, stages[j % len(stages)], hi.bitcast(F32),
                                        ALU.subtract).then_inc(stage_done, 1)
            dve.wait_ge(wg_split, 1)
            nc.vector.tensor_tensor(wg_lo[:], wg_f[:], wg_hi[:].bitcast(F32),
                                    ALU.subtract).then_inc(wg_split, 1)
            dve.wait_ge(small_in, 96)

            def carry_wait():
                nc.vector.memset(waiter[:], 0.0)

            def layer_norm_stats(b, off, i, src):
                for t in range(NT):
                    last = nc.vector.bn_stats(bn[:, i, t, :], src[:, t, :])
                last.then_inc(ln_step[i].sem, 1)
                dve.wait_ge(ln_step[i].sem, ln_step[i].at(b, off, 1))
                carry_wait()
                for t in range(NT):
                    last = nc.vector.bn_aggr(mean_var[:, i, t, :], bn[:, i, t, :])
                last.then_inc(ln_step[i].sem, 1)
                dve.wait_ge(ln_step[i].sem, ln_step[i].at(b, off, 2))
                nc.vector.tensor_scalar(var_eps[:, i, :], mean_var[:, i, :, 1], EPS, None,
                                        ALU.add).then_inc(ln_step[i].sem, 1)

            def layer_norm_apply(b, off, i, src):
                dve.wait_ge(rstd_ready[i].sem, rstd_ready[i].at(b, off, 1))
                for t in range(NT):
                    last = nc.vector.tensor_scalar(xn[:, t, :], src[:, t, :], mean_var[:, i, t, 0:1],
                                                   rstd[:, i, t:t + 1], ALU.subtract, ALU.mult)
                last.then_inc(ln_out[i].sem, 1)

            def gates_of(b, off):
                dve.wait_ge(gate_exp.sem, gate_exp.at(b, off, 1))
                nc.vector.reciprocal(g_inv[:], g_sum[:]).then_inc(gate_step.sem, 1)
                dve.wait_ge(gate_step.sem, gate_step.at(b, off, 1))
                nc.vector.tensor_tensor(g_prob[:], g_exp[:], g_inv[:].unsqueeze(2).to_broadcast([P, NT, E]),
                                        ALU.mult).then_inc(gate_step.sem, 1)
                dve.wait_ge(gate_step.sem, gate_step.at(b, off, 2))
                carry_wait()
                for t in range(NT):
                    last = nc.vector.max(g_top[:, t, :], g_prob[:, t, :])
                last.then_inc(gate_step.sem, 1)
                dve.wait_ge(gate_step.sem, gate_step.at(b, off, 3))
                nc.vector.tensor_tensor(g_two[:], g_top[:, :, 0:1], g_top[:, :, 1:2], ALU.add)
                for t in range(NT):
                    last = nc.vector.max_index(g_idx[:, t, :], g_top[:, t, :], g_prob[:, t, :])
                last.then_inc(gate_step.sem, 1)
                dve.wait_ge(gate_step.sem, gate_step.at(b, off, 4))
                nc.vector.tensor_copy(g_idf[:], g_idx[:])
                nc.vector.reciprocal(g_rtwo[:], g_two[:]).then_inc(gate_step.sem, 1)
                dve.wait_ge(gate_step.sem, gate_step.at(b, off, 5))
                nc.vector.tensor_tensor(g_val[:], g_top[:, :, 0:2], g_rtwo[:].to_broadcast([P, NT, 2]),
                                        ALU.mult).then_inc(gate_step.sem, 1)
                dve.wait_ge(gate_step.sem, gate_step.at(b, off, 6))
                for t in range(NT):
                    for i, one_hot in enumerate((g_first, g_second)):
                        last = nc.vector.tensor_scalar(one_hot[:, t, :], iota_sb[:], g_idf[:, t, i:i + 1],
                                                       g_val[:, t, i:i + 1], ALU.is_equal, ALU.mult)
                last.then_inc(gate_step.sem, 1)
                dve.wait_ge(gate_step.sem, gate_step.at(b, off, 7))
                nc.vector.tensor_tensor(gates[:], g_first[:], g_second[:], ALU.add).then_inc(gate_step.sem, 1)

            def row_maximum(b, s, h):
                dve.wait_ge(scored.sem, scored.at(b, 0, h + 1))
                ps = score_ps[s % 2]
                if h < H:
                    nc.vector.tensor_reduce(neg_max[:, h % STATS, :], ps[:].rearrange("p (t n) -> p t n", t=NT),
                                                         AX.X, ALU.max, negate=True).then_inc(max_ready.sem, 1)
                    return
                back = next(head_in(s - i) for i in (3, 6, 9) if head_in(s - i))
                dve.wait_ge(probs_turned.sem, probs_turned.at(b, back[0], back[1] + 1))
                if h == H:
                    dve.wait_ge(mask_ready.sem, mask_ready.at(b, 0, 1))
                for t in range(NT):
                    last = nc.vector.tensor_scalar(probs[:, s % P_BUFS, t, :], ps[:, t * T:(t + 1) * T],
                                                   mask_add[:, t:t + 1], None, ALU.add, ALU.max,
                                                   accum_out=row_max[:, h % STATS, t:t + 1])
                last.then_inc(max_found.sem, 1)
                dve.wait_ge(max_found.sem, max_found.at(b, 0, h - H + 1))
                nc.vector.tensor_scalar(neg_max[:, h % STATS, :], row_max[:, h % STATS, :], -1.0, None,
                                        ALU.mult).then_inc(max_ready.sem, 1)

            def low_part(lo, ps, hi):
                return nc.vector.tensor_tensor(flat(lo), ps, flat(hi).bitcast(F32), ALU.subtract)

            def rope_products(ps):
                halves = ps.rearrange("p (t h n) -> p t h n", t=NT, h=2 * HG)
                for dst, table in ((rope_a, cos_sb), (rope_b, sin_sb)):
                    last = nc.vector.tensor_tensor(dst[:].rearrange("p t (h n) -> p t h n", h=2 * HG), halves,
                                                   table[:].unsqueeze(2).to_broadcast([P, NT, 2 * HG, HALF]),
                                                   ALU.mult)
                return last

            def unit(b, ps, kind, g, off):
                if kind == "QP":
                    dve.wait_ge(qk_projected.sem, qk_projected.at(b, off, 2 * g + 1))
                    dve.wait_ge(k_turned.sem, k_turned.at(b, off if g else off - 1, g if g else NG))
                    rope_products(ps).then_inc(rope_split.sem, 1)
                elif kind == "KP":
                    dve.wait_ge(qk_projected.sem, qk_projected.at(b, off, 2 * g + 2))
                    dve.wait_ge(q_turned.sem, q_turned.at(b, off, g + 1))
                    rope_products(ps).then_inc(rope_split.sem, 1)
                elif kind == "QT":
                    hi, lo = qT_hi[:, g % 2, :, :], qT_lo[:, g % 2, :, :]
                    dve.wait_ge(q_hi_ready.sem, q_hi_ready.at(b, off, g + 1))
                    nc.vector.scalar_tensor_tensor(flat(lo), ps, SCALE, flat(hi).bitcast(F32),
                                                   ALU.mult, ALU.subtract).then_inc(q_ready.sem, 1)
                elif kind == "KT":
                    dve.wait_ge(k_hi_ready.sem, k_hi_ready.at(b, off, g + 1))
                    low_part(kT_lo[:, g % 2, :, :], ps, kT_hi[:, g % 2, :, :]).then_inc(k_ready.sem, 1)
                elif kind == "CT":
                    dve.wait_ge(ctx_hi_ready.sem, ctx_hi_ready.at(b, off, 1))
                    low_part(ct_lo[:], ps, ct_hi[:]).then_inc(ctx_ready.sem, 1)
                elif kind == "L1":
                    dve.wait_ge(xs_hi_ready.sem, xs_hi_ready.at(b, off, 1))
                    low_part(xs_lo[:], ps, xs_hi[:]).then_inc(xs_ready.sem, 1)
                elif kind in ("L2", "L3"):
                    dve.wait_ge(xc_hi_ready.sem, xc_hi_ready.at(b, off, 1 if kind == "L2" else 2))
                    low_part(xc_lo[:], ps, xc_hi[:]).then_inc(xc_ready.sem, 1)
                elif kind == "LG":
                    dve.wait_ge(logits_done.sem, logits_done.at(b, off, 1))
                    nc.vector.tensor_reduce(g_nmax[:], ps[:, 0:NT * E].rearrange("p (t n) -> p t n", t=NT),
                                            AX.X, ALU.max, negate=True).then_inc(gate_max.sem, 1)
                elif kind == "GT":
                    dve.wait_ge(gates_turned.sem, gates_turned.at(b, off, 1))
                    nc.vector.tensor_copy(gatesT, ps[0:E, 0:T]).then_inc(gatesT_ready.sem, 1)
                elif kind == "BI":
                    dve.wait_ge(bias_done.sem, bias_done.at(b, off, 1))
                    nc.vector.tensor_tensor(flat(x1[:]), ps, flat(x1[:]), ALU.add).then_inc(bias_added.sem, 1)
                elif kind == "EX":
                    j, t = divmod(g, NT)
                    dve.wait_ge(expert_done.sem, expert_done.at(b, off, g + 1))
                    if g < NT:
                        dve.wait_ge(bias_added.sem, bias_added.at(b, off, 1))
                    else:
                        dve.wait_ge(expert_added.sem, expert_added.at(b, off, 2 * (g - NT) + 2))
                    add_expert(ps, 2 * j, t).then_inc(expert_added.sem, 1)
                    dve.wait_ge(expert_added.sem, expert_added.at(b, off, 2 * g + 1))
                    add_expert(ps, 2 * j + 1, t).then_inc(expert_added.sem, 1)

            def add_expert(ps, e, t):
                i = e % 2
                return nc.vector.scalar_tensor_tensor(x1[:, t, :], ps[:, i * D:(i + 1) * D], gates[:, t, e:e + 1],
                                                      x1[:, t, :], ALU.mult, ALU.add)

            def residual(b, off, i):
                dve.wait_ge(wo_done.sem, wo_done.at(b, off, NG * (i + 1)))
                x = (x_in, x1)[i]
                if i == 0:
                    dve.wait_ge(x_loaded.sem, x_loaded.at(b, off, 1))
                nc.vector.tensor_tensor(x[:], wo_ps[:].rearrange("p (t n) -> p t n", t=NT),
                                                         x[:], ALU.add).then_inc(resid_done[i].sem, 1)
                dve.wait_ge(resid_done[i].sem, resid_done[i].at(b, off, 1))

            def body(b):
                for s in range(SLOTS):
                    summed = head_in(s - 1)
                    if summed and exists(b, summed[0]):
                        dve.wait_ge(exp_done.sem, exp_done.at(b, summed[0], summed[1] + 1))
                        nc.vector.reciprocal(inv_sum[:, summed[1] % STATS, :],
                                                          row_sum[:, summed[1] % STATS, :]).then_inc(inv_ready.sem, 1)
                    here = head_in(s)
                    if here and exists(b, 0):
                        row_maximum(b, s, here[1])
                    if s == 18 and exists(b, 0):
                        residual(b, 0, 0)
                        layer_norm_stats(b, 0, 1, x_in)
                    if s == 8 and exists(b, -1):
                        gates_of(b, -1)
                    if s == 4 and exists(b, -1):
                        if exists(b, 0):
                            dve.wait_ge(xs_turned.sem, xs_turned.at(b, 0, 1))
                        else:
                            dve.wait_ge(xc_turned.sem, xc_turned.at(b, -1, 1))
                        layer_norm_apply(b, -1, 2, x1)
                    if s == 28 and exists(b, 1):
                        dve.wait_ge(xc_turned.sem, xc_turned.at(b, 0, 1))
                        layer_norm_apply(b, 1, 0, x_in)
                    for n, (kind, g, off) in enumerate(UNITS[s]):
                        if exists(b, off):
                            unit(b, unit_ps[unit_bank(s, n) % 2][:], kind, g, off)
                        if s == 18 and n == 0 and exists(b, 0):
                            dve.wait_ge(xc_turned.sem, xc_turned.at(b, -1, 2))
                            layer_norm_apply(b, 0, 1, x_in)
                    pair = meets_values(s)
                    if pair and pair[1] % HG == 2 and exists(b, pair[0]):
                        off, h, _ = pair
                        g = h // HG
                        dve.wait_ge(oT_hi_ready.sem, oT_hi_ready.at(b, off, g + 1))
                        nc.vector.tensor_tensor(flat(oT_lo[:]), oT_ps[:],
                                                            flat(oT_hi[:]).bitcast(F32),
                                                            ALU.subtract).then_inc(oT_ready.sem, 1)
                    if s == 17 and exists(b, 0):
                        dve.wait_ge(mask_loaded.sem, mask_loaded.at(b, 0, 1))
                        nc.vector.tensor_scalar(mask_add[:], mask_i[:], -1.0, MASK_NEG,
                                                ALU.add, ALU.mult).then_inc(mask_ready.sem, 1)
                    if s == 3 and exists(b, -1):
                        residual(b, -1, 1)
                        layer_norm_stats(b, -1, 2, x1)
                    if s == 20 and exists(b, 0):
                        dve.wait_ge(stored.sem, stored.at(b, -1, 1))
                        nc.vector.tensor_tensor(x1[:], x_in[:], bout_sb[:].unsqueeze(1).to_broadcast([P, NT, D]),
                                                ALU.add).then_inc(x_moved.sem, 1)
                    if s == 27 and exists(b, 1):
                        dve.wait_ge(x_loaded.sem, x_loaded.at(b, 1, 1))
                        layer_norm_stats(b, 1, 0, x_in)

            bodies(dve, body)

        @block.gpsimd
        def _(pool):
            nc.gpsimd.memset(neg_half[:], -0.5).then_inc(consts, 1)
            nc.gpsimd.memset(ident[:], 0.0).then_inc(consts, 1)
            pool.wait_ge(consts, 2)
            nc.gpsimd.affine_select(out=ident[:], in_=ident[:], compare_op=ALU.not_equal, fill=1.0, base=0,
                                    pattern=[[-1, P]], channel_multiplier=1).then_inc(consts, 1)

            def standard_deviation(b, off, i):
                pool.wait_ge(ln_step[i].sem, ln_step[i].at(b, off, 3))
                nc.gpsimd.tensor_tensor(rstd[:, i, :], var_eps[:, i, :], neg_half[:],
                                        ALU.pow).then_inc(rstd_ready[i].sem, 1)

            def body(b):
                for s in range(SLOTS):
                    summed = head_in(s - 1)
                    if summed and exists(b, summed[0]):
                        off, h, hs = summed
                        pool.wait_ge(inv_ready.sem, inv_ready.at(b, off, h + 1))
                        weights = probs[:, hs % P_BUFS, :, :]
                        nc.gpsimd.tensor_tensor(
                            weights, weights, inv_sum[:, h % STATS, :].unsqueeze(2).to_broadcast([P, NT, T]),
                            ALU.mult).then_inc(probs_ready.sem, 1)
                    for kind, g, off in UNITS[s]:
                        if kind in ("QP", "KP") and exists(b, off):
                            k = 2 * g + (1 if kind == "QP" else 2)
                            pool.wait_ge(rope_split.sem, rope_split.at(b, off, k))
                            a = rope_a[:].rearrange("p t (h e n) -> p (t h) e n", h=HG, e=2)
                            r = rope_b[:].rearrange("p t (h e n) -> p (t h) e n", h=HG, e=2)
                            nc.gpsimd.tensor_tensor(a[:, :, 0, :], a[:, :, 0, :], r[:, :, 1, :],
                                                    ALU.subtract)
                            nc.gpsimd.tensor_tensor(a[:, :, 1, :], a[:, :, 1, :], r[:, :, 0, :],
                                                    ALU.add).then_inc(roped.sem, 1)
                    if s == 18 and exists(b, 0):
                        standard_deviation(b, 0, 1)
                    if s == 3 and exists(b, -1):
                        standard_deviation(b, -1, 2)
                    if s == 27 and exists(b, 1):
                        standard_deviation(b, 1, 0)

            bodies(pool, body)


def rotary_tables():
    pos = np.arange(T, dtype=np.float32)
    i = np.arange(HALF, dtype=np.float32)
    cos, sin = [], []
    for scale in (1.0, 4.0, 16.0):
        freqs = (np.float32(1.0) / np.float32(10000.0 * scale) ** (np.float32(2.0) * i / np.float32(HD)))
        ang = pos[:, None] * freqs[None, :].astype(np.float32)
        cos.append(np.cos(ang))
        sin.append(np.sin(ang))
    cos = np.mean(np.stack(cos), 0, dtype=np.float32)
    sin = np.mean(np.stack(sin), 0, dtype=np.float32)

    def by_partition(a):
        return np.ascontiguousarray(a.reshape(NT, P, HALF).transpose(1, 0, 2), np.float32)

    return by_partition(cos), by_partition(sin)


def kernel(**inputs):
    import concourse.bacc as bacc
    from concourse.bass_utils import run_bass_kernel_spmd as run

    def even_first(w):
        w = np.asarray(w)
        return np.ascontiguousarray(w.reshape(D, H, HALF, 2).transpose(0, 1, 3, 2).reshape(D, H * HD))

    cos, sin = rotary_tables()
    arrays = {
        "x": inputs["x"], "ctx": inputs["ctx_1024"],
        "mask": np.asarray(inputs["mask_BxS_ik0"]).reshape(B, NT, P).transpose(0, 2, 1),
        "sq": even_first(inputs["L0_attn_Wq"]), "sk": even_first(inputs["L0_attn_Wk"]),
        "sv": inputs["L0_attn_Wv"], "so": inputs["L0_attn_Wo"],
        "cq": inputs["L0_xattn_Wq"], "ckv": inputs["L0_xattn_Wkv"], "co": inputs["L0_xattn_Wout"],
        "bout": inputs["L0_xattn_bout"],
        "wg": inputs["L0_ffn_Wg"], "we": inputs["L0_ffn_We"], "be": inputs["L0_ffn_be"],
        "cos": cos, "sin": sin,
        "iota": np.tile(np.arange(E, dtype=np.float32), (P, 1)),
    }
    arrays = {k: np.ascontiguousarray(v) for k, v in arrays.items()}
    nc = bacc.Bacc("TRN2", target_bir_lowering=False, num_devices=1,
                   dynamic_dma_scratch_size=64)
    args = [nc.dram_tensor(f"dram_{k}", a.shape, mybir.dt.from_np(a.dtype), kind="ExternalInput").ap()
            for k, a in arrays.items()]
    out = nc.dram_tensor("layer_out", (B, T, D), F32, kind="ExternalOutput").ap()
    layer(nc, *args, out)
    r = run(nc, [{f"dram_{k}": a for k, a in arrays.items()}], core_ids=[0])
    return r.results[0]["layer_out"]
```

```python
from contextlib import ExitStack

import numpy as np
import concourse.bass as bass
from concourse import mybir

F32 = mybir.dt.float32
F32R = mybir.dt.float32r
I32 = mybir.dt.int32
U32 = mybir.dt.uint32
ALU = mybir.AluOpType
ACT = mybir.ActivationFunctionType
AX = mybir.AxisListType

B, T, D = 32, 256, 256
H, HD = 16, 64
E = 8
P = 128
NT = T // P
NC = D // P
HG = 4
GW = HG * HD
NG = H // HG
NH = 2 * H
HALF = HD // 2
SCALE = HD ** -0.5
MASK_NEG = 1000000.0
EPS = 1e-5

SLOTS = 36
DRAIN = (16, 20)
P_BUFS = 3
GATE_STEPS = 8
STATS = 4


def head_in(s):
    off, s = divmod(s, SLOTS)
    if DRAIN[0] <= s < DRAIN[1]:
        return None
    return off, (s if s < DRAIN[0] else s - (DRAIN[1] - DRAIN[0])), s


def meets_values(s):
    if s % SLOTS == DRAIN[0] + 1:
        return head_in(s - 3)
    if s % 2 or s % SLOTS == DRAIN[0] + 2:
        return None
    return head_in(s - 4)


def projects(s):
    if s % SLOTS == DRAIN[0] + 2:
        return head_in(s - 4)
    pair = meets_values(s - 1)
    return pair if pair and pair[1] % HG == 2 and s % SLOTS != DRAIN[0] + 2 else None


UNITS = {s: [] for s in range(SLOTS)}
for _s, _u in (
        (0, ("QT", 1, 0)), (0, ("KP", 1, 0)), (1, ("V", 1, 0)), (2, ("KT", 1, 0)),
        (2, ("QP", 2, 0)), (4, ("QT", 2, 0)), (4, ("KP", 2, 0)), (5, ("V", 2, 0)), (6, ("KT", 2, 0)),
        (6, ("QP", 3, 0)), (8, ("QT", 3, 0)), (8, ("KP", 3, 0)), (10, ("KT", 3, 0)),
        (7, ("L3", 0, -1)), (9, ("LG", 0, -1)), (9, ("V", 3, 0)), (17, ("GT", 0, -1)),
        (12, ("EX", 0, -1)), (13, ("EX", 1, -1)), (16, ("EX", 2, -1)), (16, ("EX", 3, -1)),
        (17, ("EX", 4, -1)),
        (11, ("CT", 0, 0)), (18, ("KT", 4, 0)), (18, ("EX", 5, -1)), (18, ("KT", 5, 0)), (18, ("V", 4, 0)),
        (19, ("L2", 0, 0)), (19, ("EX", 6, -1)), (19, ("QT", 4, 0)), (19, ("V", 5, 0)),
        (20, ("EX", 7, -1)), (21, ("QT", 5, 0)), (22, ("BI", 0, -1)),
        (24, ("KT", 6, 0)), (25, ("QT", 6, 0)), (26, ("V", 6, 0)),
        (28, ("KT", 7, 0)), (29, ("QT", 7, 0)), (30, ("V", 7, 0)),
        (29, ("L1", 0, 1)), (30, ("QP", 0, 1)), (32, ("QT", 0, 1)), (32, ("KP", 0, 1)),
        (33, ("V", 0, 1)), (34, ("KT", 0, 1)), (34, ("QP", 1, 1))):
    UNITS[_s] += [_u]
FLAT = [u for s in range(SLOTS) for u in UNITS[s]]


def layer(nc, x_d, ctx_d, mask_d, sq_d, sk_d, sv_d, so_d, cq_d, ckv_d, co_d, bout_d, wg_d, we_d,
          be_d, cos_d, sin_d, iota_d, out_d):
    ctx = ExitStack()
    with ctx:
        def sb(name, shape, dt=F32):
            return ctx.enter_context(nc.sbuf_tensor(name, shape, dt))

        class Signal:

            def __init__(self, name, per, step=1):
                self.sem = ctx.enter_context(nc.semaphore(name))
                self.per, self.step = per, step

            def at(self, b, off, k):
                value = b * (self.per * self.step) + (off * self.per + k) * self.step
                return max(value, 0) if isinstance(b, int) else value

        w_hi = sb("w_hi", [P, 8, NC * H * HD], F32R)
        w_lo = sb("w_lo", [P, 8, NC * H * HD], F32R)
        we_hi = sb("we_hi", [P, NC, E * D], F32R)
        we_lo = sb("we_lo", [P, NC, E * D], F32R)
        wg_f = sb("wg_f", [P, NC, E])
        wg_hi = sb("wg_hi", [P, NC, E], F32R)
        wg_lo = sb("wg_lo", [P, NC, E], F32R)
        be_sb = sb("be_sb", [E, D])[:]
        gatesT = sb("gatesT", [E, T])[:]
        bout_sb = sb("bout_sb", [P, D])
        cos_sb = sb("cos_sb", [P, NT, HALF])
        sin_sb = sb("sin_sb", [P, NT, HALF])
        iota_sb = sb("iota_sb", [P, E])
        ident = sb("ident", [P, P])
        neg_half = sb("neg_half", [P, NT])
        minus_one = sb("minus_one", [P, NT])

        x_in = sb("x_in", [P, NT, D])
        x1 = sb("x1", [P, NT, D])
        xn = sb("xn", [P, NT, D])
        ctx_in = sb("ctx_in", [P, NT, D])
        xs_hi, xs_lo = sb("xs_hi", [P, NC, T], F32R), sb("xs_lo", [P, NC, T], F32R)
        xf_hi, xf_lo = sb("xf_hi", [P, NC, T], F32R), sb("xf_lo", [P, NC, T], F32R)
        ct_hi, ct_lo = sb("ct_hi", [P, NC, T], F32R), sb("ct_lo", [P, NC, T], F32R)
        rope_a = sb("rope_a", [P, NT, GW])
        rope_b = sb("rope_b", [P, NT, GW])
        qT_hi, qT_lo = sb("qT_hi", [P, 2, 2, T], F32R), sb("qT_lo", [P, 2, 2, T], F32R)
        kT_hi, kT_lo = sb("kT_hi", [P, 2, 2, T], F32R), sb("kT_lo", [P, 2, 2, T], F32R)
        v_sb = sb("v_sb", [P, 2, NT, GW])
        probs = sb("probs", [P, P_BUFS, NT, T])
        pT = sb("pT", [P, 2, NT, T])
        oT_hi, oT_lo = sb("oT_hi", [P, 2, T], F32R), sb("oT_lo", [P, 2, T], F32R)

        neg_max = sb("neg_max", [P, STATS, NT])
        row_max = sb("row_max", [P, STATS, NT])
        row_sum = sb("row_sum", [P, STATS, NT])
        inv_sum = sb("inv_sum", [P, STATS, NT])
        mask_i = sb("mask_i", [P, NT], I32)
        mask_add = sb("mask_add", [P, NT])
        bn = sb("bn", [P, 3, NT, 6])
        mean_var = sb("mean_var", [P, 3, NT, 2])
        var_eps = sb("var_eps", [P, 3, NT])
        rstd = sb("rstd", [P, 3, NT])
        g_nmax = sb("g_nmax", [P, NT])
        g_exp = sb("g_exp", [P, NT, E])
        g_sum = sb("g_sum", [P, NT])
        g_inv = sb("g_inv", [P, NT])
        g_prob = sb("g_prob", [P, NT, E])
        g_top = sb("g_top", [P, NT, 8])
        g_idx = sb("g_idx", [P, NT, 8], U32)
        g_idf = sb("g_idf", [P, NT, 8])
        g_two = sb("g_two", [P, NT, 1])
        g_rtwo = sb("g_rtwo", [P, NT, 1])
        g_val = sb("g_val", [P, NT, 2])
        g_first = sb("g_first", [P, NT, E])
        g_second = sb("g_second", [P, NT, E])
        gates = sb("gates", [P, NT, E])
        waiter = sb("waiter", [P, 1])

        def bank(name):
            return ctx.enter_context(nc.psum_tensor(name, [P, 512], F32))

        score_ps = [bank(f"score_ps{i}") for i in range(2)]
        pT_ps = [bank(f"pT_ps{i}") for i in range(2)]
        unit_ps = [bank(f"unit_ps{i}") for i in range(2)]
        oT_ps = bank("oT_ps")
        wo_ps = bank("wo_ps")

        stage_in = [ctx.enter_context(nc.semaphore(f"stage_in{i}")) for i in range(P_BUFS + 2)]
        small_in = ctx.enter_context(nc.semaphore("small_in"))
        stage_hi = ctx.enter_context(nc.semaphore("stage_hi"))
        stage_done = ctx.enter_context(nc.semaphore("stage_done"))
        wg_split = ctx.enter_context(nc.semaphore("wg_split"))
        consts = ctx.enter_context(nc.semaphore("consts"))
        x_loaded = Signal("x_loaded", 1, 16)
        ctx_loaded = Signal("ctx_loaded", 1, 16)
        mask_loaded = Signal("mask_loaded", 1, 16)
        stored = Signal("stored", 1, 16)
        scored = Signal("scored", NH)
        probs_turned = Signal("probs_turned", NH)
        pv_done = Signal("pv_done", NH // 2)
        wo_done = Signal("wo_done", 2 * NG)
        qk_projected = Signal("qk_projected", 2 * NG)
        v_projected = Signal("v_projected", 2 * NG)
        q_turned = Signal("q_turned", 2 * NG)
        k_turned = Signal("k_turned", 2 * NG)
        ctx_turned = Signal("ctx_turned", 1)
        xs_turned = Signal("xs_turned", 2)
        xf_turned = Signal("xf_turned", 1)
        logits_done = Signal("logits_done", 1)
        gates_turned = Signal("gates_turned", 1)
        bias_done = Signal("bias_done", 1)
        expert_done = Signal("expert_done", E)
        exp_done = Signal("exp_done", NH)
        pT_ready = Signal("pT_ready", NH)
        q_hi_ready = Signal("q_hi_ready", 2 * NG)
        k_hi_ready = Signal("k_hi_ready", 2 * NG)
        ctx_hi_ready = Signal("ctx_hi_ready", 1)
        xs_hi_ready = Signal("xs_hi_ready", 2)
        xf_hi_ready = Signal("xf_hi_ready", 1)
        oT_hi_ready = Signal("oT_hi_ready", 2 * NG)
        v_ready = Signal("v_ready", 2 * NG)
        gate_exp = Signal("gate_exp", 1)
        max_found = Signal("max_found", H)
        max_ready = Signal("max_ready", NH)
        rope_split = Signal("rope_split", 2 * NG)
        q_ready = Signal("q_ready", 2 * NG)
        k_ready = Signal("k_ready", 2 * NG)
        ctx_ready = Signal("ctx_ready", 1)
        xs_ready = Signal("xs_ready", 2)
        xf_ready = Signal("xf_ready", 1)
        oT_ready = Signal("oT_ready", 2 * NG)
        resid_done = [Signal(f"resid_done{i}", 1) for i in range(2)]
        x_moved = Signal("x_moved", 1)
        mask_ready = Signal("mask_ready", 1)
        ln_step = [Signal(f"ln_step{i}", 3) for i in range(3)]
        ln_out = [Signal(f"ln_out{i}", 1) for i in range(3)]
        gate_max = Signal("gate_max", 1)
        gate_step = Signal("gate_step", GATE_STEPS)
        gatesT_ready = Signal("gatesT_ready", 1)
        bias_added = Signal("bias_added", 1)
        expert_added = Signal("expert_added", 2 * E)
        inv_ready = Signal("inv_ready", NH)
        probs_ready = Signal("probs_ready", NH)
        roped = Signal("roped", 2 * NG)
        rope_step = Signal("rope_step", 2 * NG)
        rstd_ready = [Signal(f"rstd_ready{i}", 1) for i in range(3)]

        def exists(b, off):
            return not isinstance(b, int) or 0 <= b + off < B

        def read_signal(kind, g):
            return {"QP": (rope_split, 2 * g + 1), "KP": (rope_split, 2 * g + 2), "V": (v_ready, g + 1),
                    "QT": (q_ready, g + 1), "KT": (k_ready, g + 1), "CT": (ctx_ready, 1),
                    "L1": (xs_ready, 1), "L2": (xs_ready, 2), "L3": (xf_ready, 1), "LG": (gate_exp, 1),
                    "GT": (gatesT_ready, 1), "BI": (bias_added, 1), "EX": (expert_added, 2 * g + 2)}[kind]

        def bank_before(b, at):
            prev, back = at - 1, 0
            while back > -2:
                if prev < 0:
                    prev, back = len(FLAT) - 1, back - 1
                kind, g, off = FLAT[prev]
                if prev % 2 == at % 2 and exists(b, off + back):
                    signal, k = read_signal(kind, g)
                    return signal, off + back, k
                prev -= 1
            return stored, -1, 0

        def early_values(kind, s):
            return kind == "V" and s % 4 == 1

        def unit_bank(s, n):
            return sum(len(UNITS[i]) for i in range(s)) + n

        def flat(ap):
            return ap.rearrange("p a n -> p (a n)")

        def pieces(hi, lo):
            return ((lo[0], hi[1]), (hi[0], lo[1]), (hi[0], hi[1]))

        stages = [probs[:, i, :, :].rearrange("p a n -> p (a n)") for i in range(P_BUFS)] + \
                 [pT[:, i, :, :].rearrange("p a n -> p (a n)") for i in range(2)]

        def stage_list():
            out = []
            for m, (w, c0) in enumerate(((sq_d, 0), (sk_d, 0), (sv_d, 0), (so_d, None), (cq_d, 0),
                                         (ckv_d, 0), (ckv_d, H * HD), (co_d, None))):
                for j in range(4):
                    if c0 is None:
                        src = w[2 * j * P:(2 * j + 2) * P, :].rearrange("(c p) n -> p c n", p=P)
                    else:
                        c, n = divmod(j, 2)
                        src = w[c * P:(c + 1) * P, c0 + n * 512:c0 + (n + 1) * 512]
                    out.append((src, w_hi[:, m, j * 512:(j + 1) * 512], w_lo[:, m, j * 512:(j + 1) * 512]))
            for c in range(NC):
                for j in range(E // 2):
                    src = we_d[2 * j:2 * j + 2, c * P:(c + 1) * P, :].rearrange("e p n -> p e n")
                    out.append((src, we_hi[:, c, j * 512:(j + 1) * 512], we_lo[:, c, j * 512:(j + 1) * 512]))
            return out

        STAGES = stage_list()
        def bodies(engine, body):
            body(-1)
            body(0)
            with engine.Fori(1, B - 1) as b:
                body(b)
            body(B - 1)
            body(B)

        block = ctx.enter_context(nc.Block())

        @block.sync
        def _(sp):
            for j, (src, _, _) in enumerate(STAGES):
                slot = j % len(stages)
                if j >= len(stages):
                    sp.wait_ge(stage_done, j - len(stages) + 1)
                dst = stages[slot]
                if len(src.shape) == 3:
                    dst = dst.rearrange("p (c n) -> p c n", c=2)
                sp.dma_start(dst, src).then_inc(stage_in[slot], 16)

            def body(b):
                if exists(b, 1):
                    sp.wait_ge(ctx_turned.sem, ctx_turned.at(b, 0, 1))
                    sp.dma_start(ctx_in[:], ctx_d[b + 1].rearrange("(t p) d -> p t d", p=P)) \
                        .then_inc(ctx_loaded.sem, 16)
                    sp.wait_ge(mask_ready.sem, mask_ready.at(b, 0, 1))
                    sp.dma_start(mask_i[:], mask_d[b + 1]).then_inc(mask_loaded.sem, 16)
                if exists(b, -1):
                    sp.wait_ge(bias_added.sem, bias_added.at(b, -1, 1))
                    sp.dma_start(out_d[b - 1].rearrange("(t p) d -> p t d", p=P), x1[:]).then_inc(stored.sem, 16)
                if exists(b, 1):
                    sp.wait_ge(x_moved.sem, x_moved.at(b, 0, 1))
                    sp.dma_start(x_in[:], x_d[b + 1].rearrange("(t p) d -> p t d", p=P)).then_inc(x_loaded.sem, 16)

            bodies(sp, body)
            sp.wait_ge(stored.sem, 16 * B)

        @block.tensor
        def _(pe):
            pe.wait_ge(stage_done, len(STAGES))
            pe.wait_ge(wg_split, 2)
            pe.wait_ge(consts, 4)

            def token_major(ps, src_hi, src_lo, m, g):
                for t in range(NT):
                    n = 0
                    for c in range(NC):
                        for a, w in pieces((src_hi, w_hi), (src_lo, w_lo)):
                            cols = c * H * HD + g * GW
                            last = nc.tensor.matmul(ps[:, t * GW:(t + 1) * GW], a[:, c, t * P:(t + 1) * P],
                                                    w[:, m, cols:cols + GW], start=n == 0, stop=n == 3 * NC - 1)
                            n += 1
                return last

            def dim_major(ps, src_hi, src_lo, m, g):
                for j in range(2):
                    n = 0
                    for c in range(NC):
                        for w, a in pieces((w_hi, src_hi), (w_lo, src_lo)):
                            cols = c * H * HD + g * GW + j * P
                            last = nc.tensor.matmul(ps[:, j * T:(j + 1) * T], w[:, m, cols:cols + P],
                                                    a[:, c, :], start=n == 0, stop=n == 3 * NC - 1)
                            n += 1
                return last

            def tile_product(ps, t, w_hi_, w_lo_, c0, width):
                i = 0
                for c in range(NC):
                    for a, w in pieces((xf_hi, w_hi_), (xf_lo, w_lo_)):
                        last = nc.tensor.matmul(ps, a[:, c, t * P:(t + 1) * P], w[:, c, c0:c0 + width],
                                                start=i == 0, stop=i == 3 * NC - 1)
                        i += 1
                return last

            def turn(ps, src):
                for c in range(2):
                    for t in range(NT):
                        last = nc.tensor.transpose(ps[:, c * T + t * P:c * T + (t + 1) * P],
                                                   src[:, t, c * P:(c + 1) * P], ident[:])
                return last

            def unit(b, s, n, kind, g, off):
                at = unit_bank(s, n)
                ps = unit_ps[at % 2]
                before, boff, k = bank_before(b, at)
                pe.wait_ge(before.sem, before.at(b, boff, k))
                if kind in ("QP", "KP"):
                    pe.wait_ge(xs_ready.sem, xs_ready.at(b, off, 1))
                    token_major(ps, xs_hi, xs_lo, 0 if kind == "QP" else 1, g).then_inc(qk_projected.sem, 1)
                elif kind == "V" and g < NG:
                    pe.wait_ge(xs_ready.sem, xs_ready.at(b, off, 1))
                    token_major(ps, xs_hi, xs_lo, 2, g).then_inc(v_projected.sem, 1)
                elif kind == "V":
                    pe.wait_ge(ctx_ready.sem, ctx_ready.at(b, off, 1))
                    token_major(ps, ct_hi, ct_lo, 6, g - NG).then_inc(v_projected.sem, 1)
                elif kind == "QT" and g < NG:
                    pe.wait_ge(roped.sem, roped.at(b, off, 2 * g + 1))
                    turn(ps, rope_a).then_inc(q_turned.sem, 1)
                elif kind == "KT" and g < NG:
                    pe.wait_ge(roped.sem, roped.at(b, off, 2 * g + 2))
                    turn(ps, rope_a).then_inc(k_turned.sem, 1)
                elif kind == "QT":
                    pe.wait_ge(xs_ready.sem, xs_ready.at(b, off, 2))
                    dim_major(ps, xs_hi, xs_lo, 4, g - NG).then_inc(q_turned.sem, 1)
                elif kind == "KT":
                    pe.wait_ge(ctx_ready.sem, ctx_ready.at(b, off, 1))
                    dim_major(ps, ct_hi, ct_lo, 5, g - NG).then_inc(k_turned.sem, 1)
                elif kind == "CT":
                    pe.wait_ge(ctx_loaded.sem, ctx_loaded.at(b, off, 1))
                    turn(ps, ctx_in).then_inc(ctx_turned.sem, 1)
                elif kind in ("L1", "L2"):
                    i = 0 if kind == "L1" else 1
                    pe.wait_ge(ln_out[i].sem, ln_out[i].at(b, off, 1))
                    turn(ps, xn).then_inc(xs_turned.sem, 1)
                elif kind == "L3":
                    pe.wait_ge(ln_out[2].sem, ln_out[2].at(b, off, 1))
                    turn(ps, xn).then_inc(xf_turned.sem, 1)
                elif kind == "LG":
                    pe.wait_ge(xf_ready.sem, xf_ready.at(b, off, 1))
                    for t in range(NT):
                        last = tile_product(ps[:, t * E:(t + 1) * E], t, wg_hi, wg_lo, 0, E)
                    last.then_inc(logits_done.sem, 1)
                elif kind == "GT":
                    pe.wait_ge(gate_step.sem, gate_step.at(b, off, GATE_STEPS))
                    for t in range(NT):
                        last = nc.tensor.transpose(ps[0:E, t * P:(t + 1) * P], gates[:, t, :], ident[:])
                    last.then_inc(gates_turned.sem, 1)
                elif kind == "BI":
                    pe.wait_ge(gatesT_ready.sem, gatesT_ready.at(b, off, 1))
                    for t in range(NT):
                        last = nc.tensor.matmul(ps[:, t * D:(t + 1) * D], gatesT[:, t * P:(t + 1) * P],
                                                be_sb, start=True, stop=True)
                    last.then_inc(bias_done.sem, 1)
                else:
                    j, t = divmod(g, NT)
                    tile_product(ps[:], t, we_hi, we_lo, 2 * j * D, 2 * D).then_inc(expert_done.sem, 1)

            def scores(b, s, h):
                g, hl = divmod(h, HG)
                back = next(head_in(s - i) for i in (2, 4, 6, 8) if head_in(s - i))
                read = exp_done if back[1] < H else max_ready
                pe.wait_ge(read.sem, read.at(b, back[0], back[1] + 1))
                if hl == 0:
                    pe.wait_ge(q_ready.sem, q_ready.at(b, 0, g + 1))
                    pe.wait_ge(k_ready.sem, k_ready.at(b, 0, g + 1))
                r, c = HD * (hl % 2), hl // 2
                for t in range(NT):
                    for i, (q, k) in enumerate(pieces((qT_hi, kT_hi), (qT_lo, kT_lo))):
                        last = nc.tensor.matmul(score_ps[s % 2][:, t * T:(t + 1) * T],
                                                q[r:r + HD, g % 2, c, t * P:(t + 1) * P],
                                                k[r:r + HD, g % 2, c, :], start=i == 0, stop=i == 2)
                last.then_inc(scored.sem, 1)

            def turn_probs(b, s):
                off, h, hs = head_in(s - 2)
                if not exists(b, off):
                    return
                back = next(head_in(s - 2 - i) for i in (2, 4, 6, 8) if head_in(s - 2 - i))
                pe.wait_ge(pT_ready.sem, pT_ready.at(b, back[0], back[1] + 1))
                pe.wait_ge(probs_ready.sem, probs_ready.at(b, off, h + 1))
                for k in range(NT):
                    for t in range(NT):
                        last = nc.tensor.transpose(pT_ps[s % 2][:, k * T + t * P:k * T + (t + 1) * P],
                                                   probs[:, hs % P_BUFS, t, k * P:(k + 1) * P], ident[:])
                last.then_inc(probs_turned.sem, 1)

            def values(b, s):
                off, h, hs = meets_values(s)
                if not exists(b, off):
                    return
                g, hl = divmod(h, HG)
                pe.wait_ge(pT_ready.sem, pT_ready.at(b, off, h + 2))
                if hl == 0:
                    pe.wait_ge(v_ready.sem, v_ready.at(b, off, g + 1))
                    pe.wait_ge(oT_ready.sem, oT_ready.at(b, off, g))
                for k in range(NT):
                    for i in range(2):
                        slot = (hs + i) % 2
                        last = nc.tensor.matmul(oT_ps[i * HD:(i + 1) * HD, (hl // 2) * T:(hl // 2 + 1) * T],
                                                v_sb[:, g % 2, k, (hl + i) * HD:(hl + i + 1) * HD],
                                                pT[:, slot, k, :], start=k == 0, stop=k == NT - 1,
                                                skip_group_check=True)
                last.then_inc(pv_done.sem, 1)

            def project(b, s):
                off, h, _ = projects(s)
                if not exists(b, off):
                    return
                g = h // HG
                if g == 0:
                    pe.wait_ge(resid_done[1].sem, resid_done[1].at(b, off - 1, 1))
                if g == NG:
                    pe.wait_ge(resid_done[0].sem, resid_done[0].at(b, off, 1))
                pe.wait_ge(oT_ready.sem, oT_ready.at(b, off, g + 1))
                m = 3 if g < NG else 7
                gg = g % NG
                for t in range(NT):
                    for c in range(2):
                        for i, (o, w) in enumerate(pieces((oT_hi, w_hi), (oT_lo, w_lo))):
                            cols = (2 * gg + c) * D
                            last = nc.tensor.matmul(wo_ps[:, t * D:(t + 1) * D], o[:, c, t * P:(t + 1) * P],
                                                    w[:, m, cols:cols + D],
                                                    start=gg == 0 and t == 0 and c == 0 and i == 0,
                                                    stop=gg == NG - 1 and c == 1 and i == 2,
                                                    skip_group_check=True)
                last.then_inc(wo_done.sem, 1)

            def body(b):
                for s in range(SLOTS):
                    if head_in(s) and exists(b, 0):
                        scores(b, s, head_in(s)[1])
                    if meets_values(s) and s != DRAIN[0] + 1:
                        values(b, s)
                    if head_in(s - 2):
                        turn_probs(b, s)
                    for n, (kind, g, off) in enumerate(UNITS[s]):
                        if exists(b, off):
                            unit(b, s, n, kind, g, off)
                        if s == DRAIN[0] + 2 and n == 0:
                            project(b, s)
                    if s == DRAIN[0] + 1:
                        values(b, s)
                    if projects(s) and s != DRAIN[0] + 2:
                        project(b, s)

            bodies(pe, body)

        @block.scalar
        def _(act):
            for dst, src in ((wg_f[:], wg_d.rearrange("(c p) e -> p c e", p=P)), (be_sb, be_d),
                             (bout_sb[:], bout_d.partition_broadcast(P)), (iota_sb[:], iota_d),
                             (cos_sb[:], cos_d), (sin_sb[:], sin_d)):
                act.dma_start(dst, src).then_inc(small_in, 16)
            for j, (_, hi, _) in enumerate(STAGES):
                act.wait_ge(stage_in[j % len(stages)], 16 * (j // len(stages) + 1))
                nc.scalar.activation(hi, stages[j % len(stages)], ACT.Copy).then_inc(stage_hi, 1)
            act.wait_ge(small_in, 96)
            nc.scalar.activation(wg_hi[:], wg_f[:], ACT.Copy).then_inc(wg_split, 1)
            act.wait_ge(stage_done, len(STAGES))

            def unit(b, ps, kind, g, off):
                if kind == "V":
                    act.wait_ge(v_projected.sem, v_projected.at(b, off, g + 1))
                    act.wait_ge(pv_done.sem, pv_done.at(b, off if g > 1 else off - 1, 2 * ((g - 2) % (2 * NG)) + 2))
                    nc.scalar.activation(flat(v_sb[:, g % 2, :, :]), ps, ACT.Copy).then_inc(v_ready.sem, 1)
                elif kind == "QT":
                    act.wait_ge(q_turned.sem, q_turned.at(b, off, g + 1))
                    nc.scalar.activation(flat(qT_hi[:, g % 2, :, :]), ps, ACT.Copy,
                                         scale=SCALE).then_inc(q_hi_ready.sem, 1)
                elif kind == "KT":
                    act.wait_ge(k_turned.sem, k_turned.at(b, off, g + 1))
                    nc.scalar.activation(flat(kT_hi[:, g % 2, :, :]), ps, ACT.Copy).then_inc(k_hi_ready.sem, 1)
                elif kind == "CT":
                    act.wait_ge(ctx_turned.sem, ctx_turned.at(b, off, 1))
                    nc.scalar.activation(flat(ct_hi[:]), ps, ACT.Copy).then_inc(ctx_hi_ready.sem, 1)
                elif kind in ("L1", "L2"):
                    act.wait_ge(xs_turned.sem, xs_turned.at(b, off, 1 if kind == "L1" else 2))
                    nc.scalar.activation(flat(xs_hi[:]), ps, ACT.Copy).then_inc(xs_hi_ready.sem, 1)
                elif kind == "L3":
                    act.wait_ge(xf_turned.sem, xf_turned.at(b, off, 1))
                    nc.scalar.activation(flat(xf_hi[:]), ps, ACT.Copy).then_inc(xf_hi_ready.sem, 1)
                elif kind == "LG":
                    act.wait_ge(gate_max.sem, gate_max.at(b, off, 1))
                    for t in range(NT):
                        last = nc.scalar.activation(g_exp[:, t, :], ps[:, t * E:(t + 1) * E], ACT.Exp,
                                                    bias=g_nmax[:, t:t + 1], accum_out=g_sum[:, t:t + 1])
                    last.then_inc(gate_exp.sem, 1)

            def pT_out(b, s):
                off, h, _ = head_in(s - 2)
                if not exists(b, off):
                    return
                back = next(head_in(s - 2 - i) for i in (2, 4, 6, 8) if head_in(s - 2 - i))
                act.wait_ge(pv_done.sem, pv_done.at(b, back[0], back[1] // 2 + 1))
                act.wait_ge(probs_turned.sem, probs_turned.at(b, off, h + 1))
                nc.scalar.activation(flat(pT[:, s % 2, :, :]), pT_ps[s % 2][:], ACT.Copy).then_inc(pT_ready.sem, 1)

            def exponentials(b, s, h):
                back = next(head_in(s - i) for i in (3, 6, 9) if head_in(s - i))
                act.wait_ge(probs_turned.sem, probs_turned.at(b, back[0], back[1] + 1))
                act.wait_ge(max_ready.sem, max_ready.at(b, 0, h + 1))
                for t in range(NT):
                    dst = probs[:, s % P_BUFS, t, :]
                    src = score_ps[s % 2][:, t * T:(t + 1) * T] if h < H else dst
                    last = nc.scalar.activation(dst, src, ACT.Exp, bias=neg_max[:, h % STATS, t:t + 1],
                                                accum_out=row_sum[:, h % STATS, t:t + 1])
                last.then_inc(exp_done.sem, 1)

            def oT_out(b, s):
                off, h, _ = meets_values(s)
                act.wait_ge(pv_done.sem, pv_done.at(b, off, h // 2 + 1))
                nc.scalar.activation(flat(oT_hi[:]), oT_ps[:], ACT.Copy).then_inc(oT_hi_ready.sem, 1)

            def body(b):
                for s in range(SLOTS):
                    here, pair = head_in(s), meets_values(s)
                    group_ends = pair and pair[1] % HG == 2 and exists(b, pair[0])
                    for n, (kind, g, off) in enumerate(UNITS.get(s - 1, ())):
                        if exists(b, off) and early_values(kind, s - 1):
                            unit(b, unit_ps[unit_bank(s - 1, n) % 2][:], kind, g, off)
                    if group_ends and s != DRAIN[0] + 1:
                        oT_out(b, s)
                    early = s % 2 == 0 and here and here[1] < H
                    if early and exists(b, 0):
                        exponentials(b, s, here[1])
                    if head_in(s - 2):
                        pT_out(b, s)
                    first = not early and UNITS[s] and UNITS[s][0][0] in ("QT", "KT") and UNITS[s][0][1] < NG
                    if first and exists(b, UNITS[s][0][2]):
                        unit(b, unit_ps[unit_bank(s, 0) % 2][:], *UNITS[s][0])
                    if here and not early and exists(b, 0):
                        exponentials(b, s, here[1])
                    for n, (kind, g, off) in enumerate(UNITS[s]):
                        if exists(b, off) and not early_values(kind, s) and not (first and n == 0):
                            unit(b, unit_ps[unit_bank(s, n) % 2][:], kind, g, off)
                    if group_ends and s == DRAIN[0] + 1:
                        oT_out(b, s)

            bodies(act, body)

        @block.vector
        def _(dve):
            for j, (_, hi, lo) in enumerate(STAGES):
                dve.wait_ge(stage_hi, j + 1)
                nc.vector.tensor_tensor(lo, stages[j % len(stages)], hi.bitcast(F32),
                                        ALU.subtract).then_inc(stage_done, 1)
            dve.wait_ge(wg_split, 1)
            nc.vector.tensor_tensor(wg_lo[:], wg_f[:], wg_hi[:].bitcast(F32),
                                    ALU.subtract).then_inc(wg_split, 1)
            dve.wait_ge(small_in, 96)

            def carry_wait():
                nc.vector.memset(waiter[:], 0.0)

            def layer_norm_stats(b, off, i, src):
                for t in range(NT):
                    last = nc.vector.bn_stats(bn[:, i, t, :], src[:, t, :])
                last.then_inc(ln_step[i].sem, 1)
                dve.wait_ge(ln_step[i].sem, ln_step[i].at(b, off, 1))
                carry_wait()
                for t in range(NT):
                    last = nc.vector.bn_aggr(mean_var[:, i, t, :], bn[:, i, t, :])
                last.then_inc(ln_step[i].sem, 1)
                dve.wait_ge(ln_step[i].sem, ln_step[i].at(b, off, 2))
                nc.vector.tensor_scalar(var_eps[:, i, :], mean_var[:, i, :, 1], EPS, None,
                                        ALU.add).then_inc(ln_step[i].sem, 1)

            def layer_norm_apply(b, off, i, src):
                dve.wait_ge(rstd_ready[i].sem, rstd_ready[i].at(b, off, 1))
                for t in range(NT):
                    last = nc.vector.tensor_scalar(xn[:, t, :], src[:, t, :], mean_var[:, i, t, 0:1],
                                                   rstd[:, i, t:t + 1], ALU.subtract, ALU.mult)
                last.then_inc(ln_out[i].sem, 1)

            def gate_weights(b, off):
                dve.wait_ge(gate_exp.sem, gate_exp.at(b, off, 1))
                nc.vector.reciprocal(g_inv[:], g_sum[:]).then_inc(gate_step.sem, 1)
                dve.wait_ge(gate_step.sem, gate_step.at(b, off, 1))
                nc.vector.tensor_tensor(g_prob[:], g_exp[:], g_inv[:].unsqueeze(2).to_broadcast([P, NT, E]),
                                        ALU.mult).then_inc(gate_step.sem, 1)
                dve.wait_ge(gate_step.sem, gate_step.at(b, off, 2))
                carry_wait()
                for t in range(NT):
                    last = nc.vector.max(g_top[:, t, :], g_prob[:, t, :])
                last.then_inc(gate_step.sem, 1)
                dve.wait_ge(gate_step.sem, gate_step.at(b, off, 3))
                nc.vector.tensor_tensor(g_two[:], g_top[:, :, 0:1], g_top[:, :, 1:2], ALU.add)
                for t in range(NT):
                    last = nc.vector.max_index(g_idx[:, t, :], g_top[:, t, :], g_prob[:, t, :])
                last.then_inc(gate_step.sem, 1)

            def gate_table(b, off):
                dve.wait_ge(gate_step.sem, gate_step.at(b, off, 4))
                nc.vector.tensor_copy(g_idf[:], g_idx[:])
                nc.vector.reciprocal(g_rtwo[:], g_two[:]).then_inc(gate_step.sem, 1)
                dve.wait_ge(gate_step.sem, gate_step.at(b, off, 5))
                nc.vector.tensor_tensor(g_val[:], g_top[:, :, 0:2], g_rtwo[:].to_broadcast([P, NT, 2]),
                                        ALU.mult).then_inc(gate_step.sem, 1)
                dve.wait_ge(gate_step.sem, gate_step.at(b, off, 6))
                for t in range(NT):
                    for i, one_hot in enumerate((g_first, g_second)):
                        last = nc.vector.tensor_scalar(one_hot[:, t, :], iota_sb[:], g_idf[:, t, i:i + 1],
                                                       g_val[:, t, i:i + 1], ALU.is_equal, ALU.mult)
                last.then_inc(gate_step.sem, 1)
                dve.wait_ge(gate_step.sem, gate_step.at(b, off, 7))
                nc.vector.tensor_tensor(gates[:], g_first[:], g_second[:], ALU.add).then_inc(gate_step.sem, 1)

            def row_maximum(b, s, h):
                dve.wait_ge(scored.sem, scored.at(b, 0, h + 1))
                ps = score_ps[s % 2]
                if h < H:
                    nc.vector.tensor_reduce(neg_max[:, h % STATS, :], ps[:].rearrange("p (t n) -> p t n", t=NT),
                                                         AX.X, ALU.max, negate=True).then_inc(max_ready.sem, 1)
                    return
                back = next(head_in(s - i) for i in (3, 6, 9) if head_in(s - i))
                dve.wait_ge(probs_turned.sem, probs_turned.at(b, back[0], back[1] + 1))
                if h == H:
                    dve.wait_ge(mask_ready.sem, mask_ready.at(b, 0, 1))
                for t in range(NT):
                    last = nc.vector.tensor_scalar(probs[:, s % P_BUFS, t, :], ps[:, t * T:(t + 1) * T],
                                                   mask_add[:, t:t + 1], None, ALU.add, ALU.max,
                                                   accum_out=row_max[:, h % STATS, t:t + 1])
                last.then_inc(max_found.sem, 1)
                dve.wait_ge(max_found.sem, max_found.at(b, 0, h - H + 1))
                nc.vector.tensor_scalar(neg_max[:, h % STATS, :], row_max[:, h % STATS, :], -1.0, None,
                                        ALU.mult).then_inc(max_ready.sem, 1)

            def low_part(lo, ps, hi):
                return nc.vector.tensor_tensor(flat(lo), ps, flat(hi).bitcast(F32), ALU.subtract)

            def rope_products(ps):
                halves = ps.rearrange("p (t h n) -> p t h n", t=NT, h=2 * HG)
                for dst, table in ((rope_a, cos_sb), (rope_b, sin_sb)):
                    last = nc.vector.tensor_tensor(dst[:].rearrange("p t (h n) -> p t h n", h=2 * HG), halves,
                                                   table[:].unsqueeze(2).to_broadcast([P, NT, 2 * HG, HALF]),
                                                   ALU.mult)
                return last

            def unit(b, ps, kind, g, off):
                if kind == "QP":
                    dve.wait_ge(qk_projected.sem, qk_projected.at(b, off, 2 * g + 1))
                    dve.wait_ge(k_turned.sem, k_turned.at(b, off if g else off - 1, g if g else NG))
                    rope_products(ps).then_inc(rope_split.sem, 1)
                elif kind == "KP":
                    dve.wait_ge(qk_projected.sem, qk_projected.at(b, off, 2 * g + 2))
                    dve.wait_ge(q_turned.sem, q_turned.at(b, off, g + 1))
                    rope_products(ps).then_inc(rope_split.sem, 1)
                elif kind == "QT":
                    hi, lo = qT_hi[:, g % 2, :, :], qT_lo[:, g % 2, :, :]
                    dve.wait_ge(q_hi_ready.sem, q_hi_ready.at(b, off, g + 1))
                    nc.vector.scalar_tensor_tensor(flat(lo), ps, SCALE, flat(hi).bitcast(F32),
                                                   ALU.mult, ALU.subtract).then_inc(q_ready.sem, 1)
                elif kind == "KT":
                    dve.wait_ge(k_hi_ready.sem, k_hi_ready.at(b, off, g + 1))
                    low_part(kT_lo[:, g % 2, :, :], ps, kT_hi[:, g % 2, :, :]).then_inc(k_ready.sem, 1)
                elif kind == "CT":
                    dve.wait_ge(ctx_hi_ready.sem, ctx_hi_ready.at(b, off, 1))
                    low_part(ct_lo[:], ps, ct_hi[:]).then_inc(ctx_ready.sem, 1)
                elif kind in ("L1", "L2"):
                    dve.wait_ge(xs_hi_ready.sem, xs_hi_ready.at(b, off, 1 if kind == "L1" else 2))
                    low_part(xs_lo[:], ps, xs_hi[:]).then_inc(xs_ready.sem, 1)
                elif kind == "L3":
                    dve.wait_ge(xf_hi_ready.sem, xf_hi_ready.at(b, off, 1))
                    low_part(xf_lo[:], ps, xf_hi[:]).then_inc(xf_ready.sem, 1)
                elif kind == "LG":
                    dve.wait_ge(logits_done.sem, logits_done.at(b, off, 1))
                    nc.vector.tensor_reduce(g_nmax[:], ps[:, 0:NT * E].rearrange("p (t n) -> p t n", t=NT),
                                            AX.X, ALU.max, negate=True).then_inc(gate_max.sem, 1)
                elif kind == "GT":
                    dve.wait_ge(gates_turned.sem, gates_turned.at(b, off, 1))
                    nc.vector.tensor_copy(gatesT, ps[0:E, 0:T]).then_inc(gatesT_ready.sem, 1)
                elif kind == "BI":
                    dve.wait_ge(bias_done.sem, bias_done.at(b, off, 1))
                    dve.wait_ge(expert_added.sem, expert_added.at(b, off, 2 * E))
                    nc.vector.tensor_tensor(flat(x1[:]), ps, flat(x1[:]), ALU.add).then_inc(bias_added.sem, 1)
                elif kind == "EX":
                    j, t = divmod(g, NT)
                    dve.wait_ge(expert_done.sem, expert_done.at(b, off, g + 1))
                    if g < NT:
                        dve.wait_ge(gate_step.sem, gate_step.at(b, off, GATE_STEPS))
                    else:
                        dve.wait_ge(expert_added.sem, expert_added.at(b, off, 2 * (g - NT) + 2))
                    add_expert(ps, 2 * j, t).then_inc(expert_added.sem, 1)
                    dve.wait_ge(expert_added.sem, expert_added.at(b, off, 2 * g + 1))
                    add_expert(ps, 2 * j + 1, t).then_inc(expert_added.sem, 1)

            def add_expert(ps, e, t):
                i = e % 2
                return nc.vector.scalar_tensor_tensor(x1[:, t, :], ps[:, i * D:(i + 1) * D], gates[:, t, e:e + 1],
                                                      x1[:, t, :], ALU.mult, ALU.add)

            def residual(b, off, i):
                dve.wait_ge(wo_done.sem, wo_done.at(b, off, NG * (i + 1)))
                x = (x_in, x1)[i]
                if i == 0:
                    dve.wait_ge(x_loaded.sem, x_loaded.at(b, off, 1))
                nc.vector.tensor_tensor(x[:], wo_ps[:].rearrange("p (t n) -> p t n", t=NT),
                                                         x[:], ALU.add).then_inc(resid_done[i].sem, 1)
                dve.wait_ge(resid_done[i].sem, resid_done[i].at(b, off, 1))

            def oT_low(b, s):
                off, h, _ = meets_values(s)
                g = h // HG
                dve.wait_ge(oT_hi_ready.sem, oT_hi_ready.at(b, off, g + 1))
                nc.vector.tensor_tensor(flat(oT_lo[:]), oT_ps[:], flat(oT_hi[:]).bitcast(F32),
                                        ALU.subtract).then_inc(oT_ready.sem, 1)

            def body(b):
                for s in range(SLOTS):
                    here = head_in(s)
                    if here and exists(b, 0):
                        row_maximum(b, s, here[1])
                    pair = meets_values(s)
                    group_ends = pair and pair[1] % HG == 2 and exists(b, pair[0])
                    if group_ends and s != DRAIN[0] + 1:
                        oT_low(b, s)
                    if s == 5 and exists(b, -1):
                        if exists(b, 0):
                            dve.wait_ge(xs_turned.sem, xs_turned.at(b, 0, 1))
                        else:
                            dve.wait_ge(xs_turned.sem, xs_turned.at(b, -1, 2))
                        layer_norm_apply(b, -1, 2, x1)
                    if s == 28 and exists(b, 1):
                        dve.wait_ge(xs_turned.sem, xs_turned.at(b, 0, 2))
                        layer_norm_apply(b, 1, 0, x_in)
                    for n, (kind, g, off) in enumerate(UNITS[s]):
                        if exists(b, off):
                            unit(b, unit_ps[unit_bank(s, n) % 2][:], kind, g, off)
                        if s == 18 and n == 0 and exists(b, 0):
                            residual(b, 0, 0)
                            layer_norm_stats(b, 0, 1, x_in)
                        if s == 18 and n == 1 and exists(b, 0):
                            dve.wait_ge(xf_turned.sem, xf_turned.at(b, -1, 1))
                            layer_norm_apply(b, 0, 1, x_in)
                    if group_ends and s == DRAIN[0] + 1:
                        oT_low(b, s)
                    if s == 10 and exists(b, -1):
                        gate_weights(b, -1)
                    if s == 11 and exists(b, -1):
                        gate_table(b, -1)
                    if s == 17 and exists(b, 0):
                        dve.wait_ge(mask_loaded.sem, mask_loaded.at(b, 0, 1))
                        nc.vector.tensor_scalar(mask_add[:], mask_i[:], -1.0, MASK_NEG,
                                                ALU.add, ALU.mult).then_inc(mask_ready.sem, 1)
                    if s == 3 and exists(b, -1):
                        residual(b, -1, 1)
                        layer_norm_stats(b, -1, 2, x1)
                    if s == 25 and exists(b, 0):
                        dve.wait_ge(stored.sem, stored.at(b, -1, 1))
                        nc.vector.tensor_tensor(x1[:], x_in[:], bout_sb[:].unsqueeze(1).to_broadcast([P, NT, D]),
                                                ALU.add).then_inc(x_moved.sem, 1)
                    if s == 27 and exists(b, 1):
                        dve.wait_ge(x_loaded.sem, x_loaded.at(b, 1, 1))
                        layer_norm_stats(b, 1, 0, x_in)

            bodies(dve, body)

        @block.gpsimd
        def _(pool):
            nc.gpsimd.memset(neg_half[:], -0.5).then_inc(consts, 1)
            nc.gpsimd.memset(minus_one[:], -1.0).then_inc(consts, 1)
            nc.gpsimd.memset(ident[:], 0.0).then_inc(consts, 1)
            pool.wait_ge(consts, 3)
            nc.gpsimd.affine_select(out=ident[:], in_=ident[:], compare_op=ALU.not_equal, fill=1.0, base=0,
                                    pattern=[[-1, P]], channel_multiplier=1).then_inc(consts, 1)

            def standard_deviation(b, off, i):
                pool.wait_ge(ln_step[i].sem, ln_step[i].at(b, off, 3))
                nc.gpsimd.tensor_tensor(rstd[:, i, :], var_eps[:, i, :], neg_half[:],
                                        ALU.pow).then_inc(rstd_ready[i].sem, 1)

            def body(b):
                for s in range(SLOTS):
                    summed = head_in(s - 1)
                    if summed and exists(b, summed[0]):
                        off, h, hs = summed
                        inv = inv_sum[:, h % STATS, :]
                        pool.wait_ge(exp_done.sem, exp_done.at(b, off, h + 1))
                        nc.gpsimd.tensor_tensor(inv, row_sum[:, h % STATS, :], minus_one[:], ALU.pow).then_inc(inv_ready.sem, 1)
                        pool.wait_ge(inv_ready.sem, inv_ready.at(b, off, h + 1))
                        weights = probs[:, hs % P_BUFS, :, :]
                        nc.gpsimd.tensor_tensor(
                            weights, weights, inv.unsqueeze(2).to_broadcast([P, NT, T]),
                            ALU.mult).then_inc(probs_ready.sem, 1)
                    for kind, g, off in UNITS.get(s - 1, ()):
                        if kind in ("QP", "KP") and exists(b, off):
                            k = 2 * g + (1 if kind == "QP" else 2)
                            pool.wait_ge(rope_split.sem, rope_split.at(b, off, k))
                            a = rope_a[:].rearrange("p t (h e n) -> p (t h) e n", h=HG, e=2)
                            r = rope_b[:].rearrange("p t (h e n) -> p (t h) e n", h=HG, e=2)
                            nc.gpsimd.tensor_tensor(a[:, :, 0, :], a[:, :, 0, :], r[:, :, 1, :],
                                                    ALU.subtract)
                            nc.gpsimd.tensor_tensor(a[:, :, 1, :], a[:, :, 1, :], r[:, :, 0, :],
                                                    ALU.add).then_inc(roped.sem, 1)
                    if s == 18 and exists(b, 0):
                        standard_deviation(b, 0, 1)
                    if s == 3 and exists(b, -1):
                        standard_deviation(b, -1, 2)
                    if s == 27 and exists(b, 1):
                        standard_deviation(b, 1, 0)

            bodies(pool, body)


def rotary_tables():
    pos = np.arange(T, dtype=np.float32)
    i = np.arange(HALF, dtype=np.float32)
    cos, sin = [], []
    for scale in (1.0, 4.0, 16.0):
        freqs = (np.float32(1.0) / np.float32(10000.0 * scale) ** (np.float32(2.0) * i / np.float32(HD)))
        ang = pos[:, None] * freqs[None, :].astype(np.float32)
        cos.append(np.cos(ang))
        sin.append(np.sin(ang))
    cos = np.mean(np.stack(cos), 0, dtype=np.float32)
    sin = np.mean(np.stack(sin), 0, dtype=np.float32)

    def by_partition(a):
        return np.ascontiguousarray(a.reshape(NT, P, HALF).transpose(1, 0, 2), np.float32)

    return by_partition(cos), by_partition(sin)


def kernel(**inputs):
    import concourse.bacc as bacc
    from concourse.bass_utils import run_bass_kernel_spmd as run

    def even_first(w):
        w = np.asarray(w)
        return np.ascontiguousarray(w.reshape(D, H, HALF, 2).transpose(0, 1, 3, 2).reshape(D, H * HD))

    cos, sin = rotary_tables()
    arrays = {
        "x": inputs["x"], "ctx": inputs["ctx_1024"],
        "mask": np.asarray(inputs["mask_BxS_ik0"]).reshape(B, NT, P).transpose(0, 2, 1),
        "sq": even_first(inputs["L0_attn_Wq"]), "sk": even_first(inputs["L0_attn_Wk"]),
        "sv": inputs["L0_attn_Wv"], "so": inputs["L0_attn_Wo"],
        "cq": inputs["L0_xattn_Wq"], "ckv": inputs["L0_xattn_Wkv"], "co": inputs["L0_xattn_Wout"],
        "bout": inputs["L0_xattn_bout"],
        "wg": inputs["L0_ffn_Wg"], "we": inputs["L0_ffn_We"], "be": inputs["L0_ffn_be"],
        "cos": cos, "sin": sin,
        "iota": np.tile(np.arange(E, dtype=np.float32), (P, 1)),
    }
    arrays = {k: np.ascontiguousarray(v) for k, v in arrays.items()}
    nc = bacc.Bacc("TRN2", target_bir_lowering=False, num_devices=1,
                   dynamic_dma_scratch_size=64)
    args = [nc.dram_tensor(f"dram_{k}", a.shape, mybir.dt.from_np(a.dtype), kind="ExternalInput").ap()
            for k, a in arrays.items()]
    out = nc.dram_tensor("layer_out", (B, T, D), F32, kind="ExternalOutput").ap()
    layer(nc, *args, out)
    r = run(nc, [{f"dram_{k}": a for k, a in arrays.items()}], core_ids=[0])
    return r.results[0]["layer_out"]
```

```python
from contextlib import ExitStack

import numpy as np
import concourse.bass as bass
from concourse import mybir

F32 = mybir.dt.float32
F32R = mybir.dt.float32r
I32 = mybir.dt.int32
U32 = mybir.dt.uint32
ALU = mybir.AluOpType
ACT = mybir.ActivationFunctionType
AX = mybir.AxisListType

B, T, D = 32, 256, 256
H, HD = 16, 64
E = 8
P = 128
NT = T // P
NC = D // P
HG = 4
GW = HG * HD
NG = H // HG
NH = 2 * H
HALF = HD // 2
SCALE = HD ** -0.5
MASK_NEG = 1000000.0
EPS = 1e-5

SLOTS = 36
DRAIN = (16, 20)
P_BUFS = 3
GATE_STEPS = 8
STATS = 4


def head_in(s):
    off, s = divmod(s, SLOTS)
    if DRAIN[0] <= s < DRAIN[1]:
        return None
    return off, (s if s < DRAIN[0] else s - (DRAIN[1] - DRAIN[0])), s


def meets_values(s):
    if s % SLOTS == AT["last values"][0]:
        return head_in(s - 3)
    if s % 2 or s % SLOTS == AT["last values"][0] + 1:
        return None
    return head_in(s - 4)


def projects(s):
    if s % SLOTS == AT["last projection"][0]:
        return head_in(s - 4)
    pair = meets_values(s - 1)
    return pair if pair and pair[1] % HG == 2 else None


NOW, LATE, SOON = range(3)
UNITS = {
    0: [("QT", 1, 0, NOW), ("KP", 1, 0, NOW)],
    1: [("V", 1, 0, LATE)],
    2: [("KT", 1, 0, SOON), ("QP", 2, 0, LATE)],
    3: [],
    4: [("KP", 2, 0, NOW), ("QT", 2, 0, LATE)],
    5: [("V", 2, 0, LATE)],
    6: [("KT", 2, 0, SOON), ("QP", 3, 0, NOW)],
    7: [],
    8: [("KP", 3, 0, NOW), ("QT", 3, 0, LATE)],
    9: [("V", 3, 0, LATE), ("L3", 0, -1, LATE)],
    10: [("LG", 0, -1, NOW), ("KT", 3, 0, NOW)],
    11: [("EX", 0, -1, LATE)],
    12: [("CT", 0, 0, NOW)],
    13: [("EX", 1, -1, NOW), ("KT", 4, 0, NOW)],
    14: [],
    15: [("KT", 5, 0, LATE)],
    16: [("EX", 2, -1, NOW)],
    17: [("EX", 3, -1, NOW), ("GT", 0, -1, LATE)],
    18: [("EX", 4, -1, NOW), ("V", 4, 0, NOW), ("V", 5, 0, NOW)],
    19: [("EX", 5, -1, NOW), ("L2", 0, 0, NOW), ("QT", 4, 0, NOW), ("EX", 6, -1, NOW)],
    20: [("EX", 7, -1, NOW)],
    21: [("BI", 0, -1, NOW), ("QT", 5, 0, LATE)],
    22: [],
    23: [],
    24: [("QT", 6, 0, LATE)],
    25: [("KT", 6, 0, LATE)],
    26: [],
    27: [("KT", 7, 0, SOON)],
    28: [("V", 6, 0, NOW), ("QT", 7, 0, LATE)],
    29: [("L1", 0, 1, SOON)],
    30: [("QP", 0, 1, NOW), ("V", 7, 0, NOW)],
    31: [],
    32: [("QT", 0, 1, SOON), ("KP", 0, 1, NOW)],
    33: [("V", 0, 1, NOW)],
    34: [("QP", 1, 1, NOW), ("KT", 0, 1, NOW)],
    35: [],
}
FLAT = [u for s in range(SLOTS) for u in UNITS[s]]
AT = {
    "statistics 3": 4,
    "norm 3": 5,
    "gate weights": 11,
    "gate table": 11,
    "mask": 19,
    "statistics 2": [18, 2],
    "norm 2": [18, 2],
    "x to x1": 23,
    "statistics 1": 27,
    "norm 1": 28,
    "last values": [17, 0],
    "last projection": [18, 0],
    "exp first": [0, 2, 4, 5, 6, 8, 12, 14, 20, 28],
    "residual 3": 3,
    "projection first": [],
}


def layer(nc, x_d, ctx_d, mask_d, sq_d, sk_d, sv_d, so_d, cq_d, ckv_d, co_d, bout_d, wg_d, we_d,
          be_d, cos_d, sin_d, iota_d, out_d):
    ctx = ExitStack()
    with ctx:
        def sb(name, shape, dt=F32):
            return ctx.enter_context(nc.sbuf_tensor(name, shape, dt))

        class Signal:

            def __init__(self, name, per, step=1):
                self.sem = ctx.enter_context(nc.semaphore(name))
                self.per, self.step = per, step

            def at(self, b, off, k):
                value = b * (self.per * self.step) + (off * self.per + k) * self.step
                return max(value, 0) if isinstance(b, int) else value

        w_hi = sb("w_hi", [P, 8, NC * H * HD], F32R)
        w_lo = sb("w_lo", [P, 8, NC * H * HD], F32R)
        we_hi = sb("we_hi", [P, NC, E * D], F32R)
        we_lo = sb("we_lo", [P, NC, E * D], F32R)
        wg_f = sb("wg_f", [P, NC, E])
        wg_hi = sb("wg_hi", [P, NC, E], F32R)
        wg_lo = sb("wg_lo", [P, NC, E], F32R)
        be_sb = sb("be_sb", [E, D])[:]
        cos_sb = sb("cos_sb", [P, NT, HALF])
        sin_sb = sb("sin_sb", [P, NT, HALF])
        iota_sb = sb("iota_sb", [P, E])
        ident = sb("ident", [P, P])
        neg_half = sb("neg_half", [P, NT])
        minus_one = sb("minus_one", [P, NT])

        x_in = sb("x_in", [P, NT, D])
        x1 = sb("x1", [P, NT, D])
        xn = sb("xn", [P, NT, D])
        ctx_in = xn[:]
        xs_hi, xs_lo = sb("xs_hi", [P, NC, T], F32R), sb("xs_lo", [P, NC, T], F32R)
        xf_hi, xf_lo = sb("xf_hi", [P, NC, T], F32R), sb("xf_lo", [P, NC, T], F32R)
        ct_hi, ct_lo = sb("ct_hi", [P, NC, T], F32R), sb("ct_lo", [P, NC, T], F32R)
        rope_a = sb("rope_a", [P, NT, GW])
        rope_b = sb("rope_b", [P, NT, GW])
        gatesT, bout_sb = rope_b[0:E, 0, 0:T], rope_b[:, 1, 0:D]
        q_both = sb("q_both", [P, 2, HG, T], F32R)
        k_both = sb("k_both", [P, 2, HG, T], F32R)
        k_lo = sb("k_lo", [P, 2, 2, T], F32R)
        v_sb = sb("v_sb", [P, 2, NT, GW])
        probs = sb("probs", [P, P_BUFS, NT, T])
        pT = sb("pT", [P, 2, NT, T])
        oT_hi, oT_lo = sb("oT_hi", [P, 2, T], F32R), sb("oT_lo", [P, 2, T], F32R)

        neg_max = sb("neg_max", [P, STATS, NT])
        row_sum = sb("row_sum", [P, STATS, NT])
        inv_sum = sb("inv_sum", [P, STATS, NT])
        mask_i = sb("mask_i", [P, NT], I32)
        mask_add = sb("mask_add", [P, NT])
        bn = sb("bn", [P, 3, NT, 6])
        mean_var = sb("mean_var", [P, 3, NT, 2])
        var_eps = sb("var_eps", [P, 3, NT])
        rstd = sb("rstd", [P, 3, NT])
        g_nmax = sb("g_nmax", [P, NT])
        g_exp = sb("g_exp", [P, NT, E])
        g_sum = sb("g_sum", [P, NT])
        g_inv = sb("g_inv", [P, NT])
        g_prob = sb("g_prob", [P, NT, E])
        g_top = sb("g_top", [P, NT, 8])
        g_idx = sb("g_idx", [P, NT, 8], U32)
        g_idf = sb("g_idf", [P, NT, 8])
        g_two = sb("g_two", [P, NT, 1])
        g_rtwo = sb("g_rtwo", [P, NT, 1])
        g_val = sb("g_val", [P, NT, 2])
        g_first = sb("g_first", [P, NT, E])
        g_second = sb("g_second", [P, NT, E])
        gates = sb("gates", [P, NT, E])
        waiter = sb("waiter", [P, 1])

        def bank(name):
            return ctx.enter_context(nc.psum_tensor(name, [P, 512], F32))

        score_ps = [bank(f"score_ps{i}") for i in range(2)]
        pT_ps = [bank(f"pT_ps{i}") for i in range(2)]
        unit_ps = [bank(f"unit_ps{i}") for i in range(2)]
        oT_ps = bank("oT_ps")
        wo_ps = bank("wo_ps")

        stage_in = [ctx.enter_context(nc.semaphore(f"stage_in{i}")) for i in range(P_BUFS + 2)]
        small_in = ctx.enter_context(nc.semaphore("small_in"))
        stage_hi = ctx.enter_context(nc.semaphore("stage_hi"))
        stage_done = ctx.enter_context(nc.semaphore("stage_done"))
        wg_split = ctx.enter_context(nc.semaphore("wg_split"))
        consts = ctx.enter_context(nc.semaphore("consts"))
        x_loaded = Signal("x_loaded", 1, 16)
        bout_loaded = Signal("bout_loaded", 1, 16)
        k_copied = [Signal(f"k_copied{i}", NG // 2, 32) for i in range(2)]
        ctx_loaded = Signal("ctx_loaded", 1, 16)
        mask_loaded = Signal("mask_loaded", 1, 16)
        stored = Signal("stored", 1, 16)
        scored = Signal("scored", NH)
        probs_turned = Signal("probs_turned", NH)
        pv_done = Signal("pv_done", NH // 2)
        wo_done = Signal("wo_done", 2 * NG)
        qk_projected = Signal("qk_projected", 2 * NG)
        v_projected = Signal("v_projected", 2 * NG)
        q_turned = Signal("q_turned", 2 * NG)
        k_turned = Signal("k_turned", 2 * NG)
        ctx_turned = Signal("ctx_turned", 1)
        xs_turned = Signal("xs_turned", 2)
        xf_turned = Signal("xf_turned", 1)
        logits_done = Signal("logits_done", 1)
        gates_turned = Signal("gates_turned", 1)
        bias_done = Signal("bias_done", 1)
        expert_done = Signal("expert_done", E)
        exp_done = Signal("exp_done", NH)
        pT_ready = Signal("pT_ready", NH)
        q_hi_ready = Signal("q_hi_ready", 2 * NG)
        k_hi_ready = Signal("k_hi_ready", 2 * NG)
        ctx_hi_ready = Signal("ctx_hi_ready", 1)
        xs_hi_ready = Signal("xs_hi_ready", 2)
        xf_hi_ready = Signal("xf_hi_ready", 1)
        oT_hi_ready = Signal("oT_hi_ready", 2 * NG)
        v_ready = Signal("v_ready", 2 * NG)
        gate_exp = Signal("gate_exp", 1)
        max_ready = Signal("max_ready", NH)
        rope_split = Signal("rope_split", 2 * NG)
        q_ready = Signal("q_ready", 2 * NG)
        k_ready = Signal("k_ready", 2 * NG)
        ctx_ready = Signal("ctx_ready", 1)
        xs_ready = Signal("xs_ready", 2)
        xf_ready = Signal("xf_ready", 1)
        oT_ready = Signal("oT_ready", 2 * NG)
        resid_done = [Signal(f"resid_done{i}", 1) for i in range(2)]
        x_moved = Signal("x_moved", 1)
        mask_ready = Signal("mask_ready", 1)
        ln_step = [Signal(f"ln_step{i}", 3) for i in range(3)]
        ln_out = [Signal(f"ln_out{i}", 1) for i in range(3)]
        gate_max = Signal("gate_max", 1)
        gate_step = Signal("gate_step", GATE_STEPS)
        gatesT_ready = Signal("gatesT_ready", 1)
        bias_added = Signal("bias_added", 1)
        expert_added = Signal("expert_added", 2 * E)
        inv_ready = Signal("inv_ready", NH)
        probs_ready = Signal("probs_ready", NH)
        roped = Signal("roped", 2 * NG)
        rope_step = Signal("rope_step", 2 * NG)
        rstd_ready = [Signal(f"rstd_ready{i}", 1) for i in range(3)]

        def exists(b, off):
            return not isinstance(b, int) or 0 <= b + off < B

        def read_signal(kind, g):
            return {"QP": (rope_split, 2 * g + 1), "KP": (rope_split, 2 * g + 2), "V": (v_ready, g + 1),
                    "QT": (q_ready, g + 1), "KT": (k_ready, g + 1), "CT": (ctx_ready, 1),
                    "L1": (xs_ready, 1), "L2": (xs_ready, 2), "L3": (xf_ready, 1), "LG": (gate_exp, 1),
                    "GT": (gatesT_ready, 1), "BI": (bias_added, 1), "EX": (expert_added, 2 * g + 2)}[kind]

        def bank_before(b, at):
            prev, back = at - 1, 0
            while back > -2:
                if prev < 0:
                    prev, back = len(FLAT) - 1, back - 1
                kind, g, off, _ = FLAT[prev]
                if prev % 2 == at % 2 and exists(b, off + back):
                    signal, k = read_signal(kind, g)
                    return signal, off + back, k
                prev -= 1
            return stored, -1, 0

        def unit_bank(s, n):
            return sum(len(UNITS[i]) for i in range(s)) + n

        def half_of(ps, i):
            return ps[i * HD:(i + 1) * HD, :].rearrange("p (c n) -> p c n", c=2)

        def head_half(both, g, i, at):
            return both[at * HD:(at + 1) * HD, g % 2, :, :].rearrange("p (c i) n -> p i c n", i=2)[:, i]

        def flat(ap):
            return ap.rearrange("p a n -> p (a n)")

        def pieces(hi, lo):
            return ((lo[0], hi[1]), (hi[0], lo[1]), (hi[0], hi[1]))

        stages = [probs[:, i, :, :].rearrange("p a n -> p (a n)") for i in range(P_BUFS)] + \
                 [pT[:, i, :, :].rearrange("p a n -> p (a n)") for i in range(2)]

        def stage_list():
            out = []
            for m, (w, c0) in enumerate(((sq_d, 0), (sk_d, 0), (sv_d, 0), (so_d, None), (cq_d, 0),
                                         (ckv_d, 0), (ckv_d, H * HD), (co_d, None))):
                for j in range(4):
                    if c0 is None:
                        src = w[2 * j * P:(2 * j + 2) * P, :].rearrange("(c p) n -> p c n", p=P)
                    else:
                        c, n = divmod(j, 2)
                        src = w[c * P:(c + 1) * P, c0 + n * 512:c0 + (n + 1) * 512]
                    out.append((src, w_hi[:, m, j * 512:(j + 1) * 512], w_lo[:, m, j * 512:(j + 1) * 512]))
            for c in range(NC):
                for j in range(E // 2):
                    src = we_d[2 * j:2 * j + 2, c * P:(c + 1) * P, :].rearrange("e p n -> p e n")
                    out.append((src, we_hi[:, c, j * 512:(j + 1) * 512], we_lo[:, c, j * 512:(j + 1) * 512]))
            return out

        STAGES = stage_list()
        def bodies(engine, body):
            body(-1)
            body(0)
            with engine.Fori(1, B - 1) as b:
                body(b)
            body(B - 1)
            body(B)

        block = ctx.enter_context(nc.Block())

        @block.sync
        def _(sp):
            for j, (src, _, _) in enumerate(STAGES):
                slot = j % len(stages)
                if j >= len(stages):
                    sp.wait_ge(stage_done, j - len(stages) + 1)
                dst = stages[slot]
                if len(src.shape) == 3:
                    dst = dst.rearrange("p (c n) -> p c n", c=2)
                sp.dma_start(dst, src).then_inc(stage_in[slot], 16)

            def copy_k(b, g):
                sp.wait_ge(k_hi_ready.sem, k_hi_ready.at(b, 0, g + 1))
                for i in range(2):
                    sp.dma_start(head_half(k_both, g, i, 1 - i).bitcast(F32),
                                 head_half(k_both, g, i, i).bitcast(F32)).then_inc(k_copied[g % 2].sem, 16)

            def body(b):
                for s in range(SLOTS):
                    for kind, g, off, _ in UNITS[s]:
                        if kind == "KT" and g >= NG and exists(b, 0):
                            copy_k(b, g)
                        if kind == "L3" and exists(b, 0):
                            if exists(b, -1):
                                sp.wait_ge(xf_turned.sem, xf_turned.at(b, -1, 1))
                            else:
                                sp.wait_ge(xs_turned.sem, xs_turned.at(b, 0, 1))
                            sp.dma_start(ctx_in, ctx_d[b].rearrange("(t p) d -> p t d", p=P)) \
                                .then_inc(ctx_loaded.sem, 16)
                        if kind == "KT" and g == NG - 1 and exists(b, 0):
                            sp.wait_ge(roped.sem, roped.at(b, 0, 2 * NG))
                            sp.dma_start(bout_sb, bout_d.partition_broadcast(P)).then_inc(bout_loaded.sem, 16)
                        if kind == "BI" and exists(b, -1):
                            sp.wait_ge(bias_added.sem, bias_added.at(b, -1, 1))
                            sp.dma_start(out_d[b - 1].rearrange("(t p) d -> p t d", p=P), x1[:]) \
                                .then_inc(stored.sem, 16)
                    if s == AT["mask"] and exists(b, 1):
                        sp.wait_ge(mask_ready.sem, mask_ready.at(b, 0, 1))
                        sp.dma_start(mask_i[:], mask_d[b + 1]).then_inc(mask_loaded.sem, 16)
                    if s == AT["x to x1"] and exists(b, 1):
                        sp.wait_ge(x_moved.sem, x_moved.at(b, 0, 1))
                        sp.dma_start(x_in[:], x_d[b + 1].rearrange("(t p) d -> p t d", p=P)) \
                            .then_inc(x_loaded.sem, 16)

            bodies(sp, body)
            sp.wait_ge(stored.sem, 16 * B)

        @block.tensor
        def _(pe):
            pe.wait_ge(stage_done, len(STAGES))
            pe.wait_ge(wg_split, 2)
            pe.wait_ge(consts, 4)

            def token_major(ps, src_hi, src_lo, m, g):
                for t in range(NT):
                    n = 0
                    for c in range(NC):
                        for a, w in pieces((src_hi, w_hi), (src_lo, w_lo)):
                            cols = c * H * HD + g * GW
                            last = nc.tensor.matmul(ps[:, t * GW:(t + 1) * GW], a[:, c, t * P:(t + 1) * P],
                                                    w[:, m, cols:cols + GW], start=n == 0, stop=n == 3 * NC - 1)
                            n += 1
                return last

            def dim_major(ps, src_hi, src_lo, m, g):
                for j in range(2):
                    n = 0
                    for c in range(NC):
                        for w, a in pieces((w_hi, src_hi), (w_lo, src_lo)):
                            cols = c * H * HD + g * GW + j * P
                            last = nc.tensor.matmul(ps[:, j * T:(j + 1) * T], w[:, m, cols:cols + P],
                                                    a[:, c, :], start=n == 0, stop=n == 3 * NC - 1)
                            n += 1
                return last

            def tile_product(ps, t, w_hi_, w_lo_, c0, width):
                i = 0
                for c in range(NC):
                    for a, w in pieces((xf_hi, w_hi_), (xf_lo, w_lo_)):
                        last = nc.tensor.matmul(ps, a[:, c, t * P:(t + 1) * P], w[:, c, c0:c0 + width],
                                                start=i == 0, stop=i == 3 * NC - 1)
                        i += 1
                return last

            def turn(ps, src):
                for c in range(2):
                    for t in range(NT):
                        last = nc.tensor.transpose(ps[:, c * T + t * P:c * T + (t + 1) * P],
                                                   src[:, t, c * P:(c + 1) * P], ident[:])
                return last

            def unit(b, s, n, kind, g, off):
                at = unit_bank(s, n)
                ps = unit_ps[at % 2]
                before, boff, k = bank_before(b, at)
                pe.wait_ge(before.sem, before.at(b, boff, k))
                if kind in ("QP", "KP"):
                    pe.wait_ge(xs_ready.sem, xs_ready.at(b, off, 1))
                    token_major(ps, xs_hi, xs_lo, 0 if kind == "QP" else 1, g).then_inc(qk_projected.sem, 1)
                elif kind == "V" and g < NG:
                    pe.wait_ge(xs_ready.sem, xs_ready.at(b, off, 1))
                    token_major(ps, xs_hi, xs_lo, 2, g).then_inc(v_projected.sem, 1)
                elif kind == "V":
                    pe.wait_ge(ctx_ready.sem, ctx_ready.at(b, off, 1))
                    token_major(ps, ct_hi, ct_lo, 6, g - NG).then_inc(v_projected.sem, 1)
                elif kind == "QT" and g < NG:
                    pe.wait_ge(roped.sem, roped.at(b, off, 2 * g + 1))
                    turn(ps, rope_a).then_inc(q_turned.sem, 1)
                elif kind == "KT" and g < NG:
                    pe.wait_ge(roped.sem, roped.at(b, off, 2 * g + 2))
                    turn(ps, rope_a).then_inc(k_turned.sem, 1)
                elif kind == "QT":
                    pe.wait_ge(xs_ready.sem, xs_ready.at(b, off, 2))
                    dim_major(ps, xs_hi, xs_lo, 4, g - NG).then_inc(q_turned.sem, 1)
                elif kind == "KT":
                    pe.wait_ge(ctx_ready.sem, ctx_ready.at(b, off, 1))
                    dim_major(ps, ct_hi, ct_lo, 5, g - NG).then_inc(k_turned.sem, 1)
                elif kind == "CT":
                    pe.wait_ge(ctx_loaded.sem, ctx_loaded.at(b, off, 1))
                    turn(ps, ctx_in).then_inc(ctx_turned.sem, 1)
                elif kind in ("L1", "L2"):
                    i = 0 if kind == "L1" else 1
                    pe.wait_ge(ln_out[i].sem, ln_out[i].at(b, off, 1))
                    turn(ps, xn).then_inc(xs_turned.sem, 1)
                elif kind == "L3":
                    pe.wait_ge(ln_out[2].sem, ln_out[2].at(b, off, 1))
                    turn(ps, xn).then_inc(xf_turned.sem, 1)
                elif kind == "LG":
                    pe.wait_ge(xf_ready.sem, xf_ready.at(b, off, 1))
                    for t in range(NT):
                        last = tile_product(ps[:, t * E:(t + 1) * E], t, wg_hi, wg_lo, 0, E)
                    last.then_inc(logits_done.sem, 1)
                elif kind == "GT":
                    pe.wait_ge(gate_step.sem, gate_step.at(b, off, GATE_STEPS))
                    for t in range(NT):
                        last = nc.tensor.transpose(ps[0:E, t * P:(t + 1) * P], gates[:, t, :], ident[:])
                    last.then_inc(gates_turned.sem, 1)
                elif kind == "BI":
                    pe.wait_ge(gatesT_ready.sem, gatesT_ready.at(b, off, 1))
                    for t in range(NT):
                        last = nc.tensor.matmul(ps[:, t * D:(t + 1) * D], gatesT[:, t * P:(t + 1) * P],
                                                be_sb, start=True, stop=True)
                    last.then_inc(bias_done.sem, 1)
                else:
                    j, t = divmod(g, NT)
                    tile_product(ps[:], t, we_hi, we_lo, 2 * j * D, 2 * D).then_inc(expert_done.sem, 1)

            def scores(b, s, h):
                g, hl = divmod(h, HG)
                back = next(head_in(s - i) for i in (2, 4, 6, 8) if head_in(s - i))
                read = exp_done if back[1] < H else max_ready
                pe.wait_ge(read.sem, read.at(b, back[0], back[1] + 1))
                if hl == 0:
                    pe.wait_ge(q_ready.sem, q_ready.at(b, 0, g + 1))
                    pe.wait_ge(k_ready.sem, k_ready.at(b, 0, g + 1))
                    if g >= NG:
                        pe.wait_ge(k_copied[g % 2].sem, k_copied[g % 2].at(b, 0, (g - NG) // 2 + 1))
                r, c = HD * (hl % 2), hl // 2
                for t in range(NT):
                    ps = score_ps[s % 2][:, t * T:(t + 1) * T]
                    cols = slice(t * P, (t + 1) * P)
                    if g < NG:
                        own = slice(r, r + HD)
                        q_hi, q_lo = q_both[own, g % 2, c, cols], q_both[own, g % 2, 2 + c, cols]
                        k_hi = k_both[own, g % 2, c, :]
                        products = ((q_hi, k_lo[own, g % 2, c, :]), (q_lo, k_hi), (q_hi, k_hi))
                    else:
                        products = ((q_both[r:r + HD, g % 2, hl, cols], k_lo[r:r + HD, g % 2, c, :]),
                                    (q_both[:, g % 2, hl, cols], k_both[:, g % 2, hl, :]))
                    for i, (q, k) in enumerate(products):
                        last = nc.tensor.matmul(ps, q, k, start=i == 0, stop=i == len(products) - 1)
                last.then_inc(scored.sem, 1)

            def turn_probs(b, s):
                off, h, hs = head_in(s - 2)
                if not exists(b, off):
                    return
                back = next(head_in(s - 2 - i) for i in (2, 4, 6, 8) if head_in(s - 2 - i))
                pe.wait_ge(pT_ready.sem, pT_ready.at(b, back[0], back[1] + 1))
                pe.wait_ge(probs_ready.sem, probs_ready.at(b, off, h + 1))
                for k in range(NT):
                    for t in range(NT):
                        last = nc.tensor.transpose(pT_ps[s % 2][:, k * T + t * P:k * T + (t + 1) * P],
                                                   probs[:, hs % P_BUFS, t, k * P:(k + 1) * P], ident[:])
                last.then_inc(probs_turned.sem, 1)

            def values(b, s):
                off, h, hs = meets_values(s)
                if not exists(b, off):
                    return
                g, hl = divmod(h, HG)
                pe.wait_ge(pT_ready.sem, pT_ready.at(b, off, h + 2))
                if hl == 0:
                    pe.wait_ge(v_ready.sem, v_ready.at(b, off, g + 1))
                    pe.wait_ge(oT_ready.sem, oT_ready.at(b, off, g))
                for k in range(NT):
                    for i in range(2):
                        slot = (hs + i) % 2
                        last = nc.tensor.matmul(oT_ps[i * HD:(i + 1) * HD, (hl // 2) * T:(hl // 2 + 1) * T],
                                                v_sb[:, g % 2, k, (hl + i) * HD:(hl + i + 1) * HD],
                                                pT[:, slot, k, :], start=k == 0, stop=k == NT - 1,
                                                skip_group_check=True)
                last.then_inc(pv_done.sem, 1)

            def project(b, s):
                off, h, _ = projects(s)
                if not exists(b, off):
                    return
                g = h // HG
                if g == 0:
                    pe.wait_ge(resid_done[1].sem, resid_done[1].at(b, off - 1, 1))
                if g == NG:
                    pe.wait_ge(resid_done[0].sem, resid_done[0].at(b, off, 1))
                pe.wait_ge(oT_ready.sem, oT_ready.at(b, off, g + 1))
                m = 3 if g < NG else 7
                gg = g % NG
                for t in range(NT):
                    for c in range(2):
                        for i, (o, w) in enumerate(pieces((oT_hi, w_hi), (oT_lo, w_lo))):
                            cols = (2 * gg + c) * D
                            last = nc.tensor.matmul(wo_ps[:, t * D:(t + 1) * D], o[:, c, t * P:(t + 1) * P],
                                                    w[:, m, cols:cols + D],
                                                    start=gg == 0 and t == 0 and c == 0 and i == 0,
                                                    stop=gg == NG - 1 and c == 1 and i == 2,
                                                    skip_group_check=True)
                last.then_inc(wo_done.sem, 1)

            def body(b):
                for s in range(SLOTS):
                    if head_in(s) and exists(b, 0):
                        scores(b, s, head_in(s)[1])
                    if meets_values(s) and s != AT["last values"][0]:
                        values(b, s)
                    if head_in(s - 2):
                        turn_probs(b, s)
                    if projects(s) and s in AT["projection first"]:
                        project(b, s)
                    for n, (kind, g, off, _) in enumerate(UNITS[s]):
                        if exists(b, off):
                            unit(b, s, n, kind, g, off)
                        if [s, n] == AT["last values"]:
                            values(b, s)
                        if [s, n] == AT["last projection"]:
                            project(b, s)
                    if projects(s) and s != AT["last projection"][0] and s not in AT["projection first"]:
                        project(b, s)

            bodies(pe, body)

        @block.scalar
        def _(act):
            for dst, src in ((wg_f[:], wg_d.rearrange("(c p) e -> p c e", p=P)), (be_sb, be_d),
                             (iota_sb[:], iota_d),
                             (cos_sb[:], cos_d), (sin_sb[:], sin_d)):
                act.dma_start(dst, src).then_inc(small_in, 16)
            for j, (_, hi, _) in enumerate(STAGES):
                act.wait_ge(stage_in[j % len(stages)], 16 * (j // len(stages) + 1))
                nc.scalar.activation(hi, stages[j % len(stages)], ACT.Copy).then_inc(stage_hi, 1)
            act.wait_ge(small_in, 80)
            nc.scalar.activation(wg_hi[:], wg_f[:], ACT.Copy).then_inc(wg_split, 1)
            act.wait_ge(stage_done, len(STAGES))

            def unit(b, ps, kind, g, off):
                if kind == "V":
                    act.wait_ge(v_projected.sem, v_projected.at(b, off, g + 1))
                    act.wait_ge(pv_done.sem, pv_done.at(b, off if g > 1 else off - 1, 2 * ((g - 2) % (2 * NG)) + 2))
                    nc.scalar.activation(flat(v_sb[:, g % 2, :, :]), ps, ACT.Copy).then_inc(v_ready.sem, 1)
                elif kind == "QT":
                    act.wait_ge(q_turned.sem, q_turned.at(b, off, g + 1))
                    if g < NG:
                        last = nc.scalar.activation(flat(q_both[:, g % 2, 0:2, :]), ps, ACT.Copy, scale=SCALE)
                    else:
                        for i in range(2):
                            last = nc.scalar.activation(head_half(q_both, g, i, i), half_of(ps, i), ACT.Copy,
                                                        scale=-SCALE)
                    last.then_inc(q_hi_ready.sem, 1)
                elif kind == "KT":
                    act.wait_ge(k_turned.sem, k_turned.at(b, off, g + 1))
                    if g < NG:
                        last = nc.scalar.activation(flat(k_both[:, g % 2, 0:2, :]), ps, ACT.Copy)
                    else:
                        for i in range(2):
                            last = nc.scalar.activation(head_half(k_both, g, i, i), half_of(ps, i), ACT.Copy)
                    last.then_inc(k_hi_ready.sem, 1)
                elif kind == "CT":
                    act.wait_ge(ctx_turned.sem, ctx_turned.at(b, off, 1))
                    nc.scalar.activation(flat(ct_hi[:]), ps, ACT.Copy).then_inc(ctx_hi_ready.sem, 1)
                elif kind in ("L1", "L2"):
                    act.wait_ge(xs_turned.sem, xs_turned.at(b, off, 1 if kind == "L1" else 2))
                    nc.scalar.activation(flat(xs_hi[:]), ps, ACT.Copy).then_inc(xs_hi_ready.sem, 1)
                elif kind == "L3":
                    act.wait_ge(xf_turned.sem, xf_turned.at(b, off, 1))
                    nc.scalar.activation(flat(xf_hi[:]), ps, ACT.Copy).then_inc(xf_hi_ready.sem, 1)
                elif kind == "LG":
                    act.wait_ge(gate_max.sem, gate_max.at(b, off, 1))
                    for t in range(NT):
                        last = nc.scalar.activation(g_exp[:, t, :], ps[:, t * E:(t + 1) * E], ACT.Exp,
                                                    bias=g_nmax[:, t:t + 1], accum_out=g_sum[:, t:t + 1])
                    last.then_inc(gate_exp.sem, 1)

            def pT_out(b, s):
                off, h, _ = head_in(s - 2)
                if not exists(b, off):
                    return
                back = next(head_in(s - 2 - i) for i in (2, 4, 6, 8) if head_in(s - 2 - i))
                act.wait_ge(pv_done.sem, pv_done.at(b, back[0], back[1] // 2 + 1))
                act.wait_ge(probs_turned.sem, probs_turned.at(b, off, h + 1))
                nc.scalar.activation(flat(pT[:, s % 2, :, :]), pT_ps[s % 2][:], ACT.Copy).then_inc(pT_ready.sem, 1)

            def exponentials(b, s, h):
                back = next(head_in(s - i) for i in (3, 6, 9) if head_in(s - i))
                act.wait_ge(probs_turned.sem, probs_turned.at(b, back[0], back[1] + 1))
                act.wait_ge(max_ready.sem, max_ready.at(b, 0, h + 1))
                for t in range(NT):
                    dst = probs[:, s % P_BUFS, t, :]
                    src = score_ps[s % 2][:, t * T:(t + 1) * T] if h < H else dst
                    last = nc.scalar.activation(dst, src, ACT.Exp, bias=neg_max[:, h % STATS, t:t + 1],
                                                scale=1.0 if h < H else -1.0,
                                                accum_out=row_sum[:, h % STATS, t:t + 1])
                last.then_inc(exp_done.sem, 1)

            def oT_out(b, s):
                off, h, _ = meets_values(s)
                act.wait_ge(pv_done.sem, pv_done.at(b, off, h // 2 + 1))
                nc.scalar.activation(flat(oT_hi[:]), oT_ps[:], ACT.Copy).then_inc(oT_hi_ready.sem, 1)

            def body(b):
                for s in range(SLOTS):
                    here, pair = head_in(s), meets_values(s)
                    group_ends = pair and pair[1] % HG == 2 and exists(b, pair[0])
                    for n, (kind, g, off, late) in enumerate(UNITS.get(s - 1, ())):
                        if exists(b, off) and late == LATE and kind == "V":
                            unit(b, unit_ps[unit_bank(s - 1, n) % 2][:], kind, g, off)
                    if group_ends and s != AT["last values"][0]:
                        oT_out(b, s)
                    early = s in AT["exp first"]
                    if early and here and exists(b, 0):
                        exponentials(b, s, here[1])
                    if head_in(s - 2):
                        pT_out(b, s)
                    first = UNITS[s] and UNITS[s][0][3] == SOON
                    if first and exists(b, UNITS[s][0][2]):
                        unit(b, unit_ps[unit_bank(s, 0) % 2][:], *UNITS[s][0][:3])
                    if here and not early and exists(b, 0):
                        exponentials(b, s, here[1])
                    for n, (kind, g, off, late) in enumerate(UNITS[s]):
                        if exists(b, off) and not (late == LATE and kind == "V") and not (first and n == 0):
                            unit(b, unit_ps[unit_bank(s, n) % 2][:], kind, g, off)
                        if [s, n] == AT["last values"] and group_ends:
                            oT_out(b, s)

            bodies(act, body)

        @block.vector
        def _(dve):
            for j, (_, hi, lo) in enumerate(STAGES):
                dve.wait_ge(stage_hi, j + 1)
                nc.vector.tensor_tensor(lo, stages[j % len(stages)], hi.bitcast(F32),
                                        ALU.subtract).then_inc(stage_done, 1)
            dve.wait_ge(wg_split, 1)
            nc.vector.tensor_tensor(wg_lo[:], wg_f[:], wg_hi[:].bitcast(F32),
                                    ALU.subtract).then_inc(wg_split, 1)
            dve.wait_ge(small_in, 80)

            def carry_wait():
                nc.vector.memset(waiter[:], 0.0)

            def layer_norm_stats(b, off, i, src):
                for t in range(NT):
                    last = nc.vector.bn_stats(bn[:, i, t, :], src[:, t, :])
                last.then_inc(ln_step[i].sem, 1)
                dve.wait_ge(ln_step[i].sem, ln_step[i].at(b, off, 1))
                carry_wait()
                for t in range(NT):
                    last = nc.vector.bn_aggr(mean_var[:, i, t, :], bn[:, i, t, :])
                last.then_inc(ln_step[i].sem, 1)
                dve.wait_ge(ln_step[i].sem, ln_step[i].at(b, off, 2))
                nc.vector.tensor_scalar(var_eps[:, i, :], mean_var[:, i, :, 1], EPS, None,
                                        ALU.add).then_inc(ln_step[i].sem, 1)

            def layer_norm_apply(b, off, i, src):
                dve.wait_ge(rstd_ready[i].sem, rstd_ready[i].at(b, off, 1))
                for t in range(NT):
                    last = nc.vector.tensor_scalar(xn[:, t, :], src[:, t, :], mean_var[:, i, t, 0:1],
                                                   rstd[:, i, t:t + 1], ALU.subtract, ALU.mult)
                last.then_inc(ln_out[i].sem, 1)

            def gate_weights(b, off):
                dve.wait_ge(gate_exp.sem, gate_exp.at(b, off, 1))
                nc.vector.reciprocal(g_inv[:], g_sum[:]).then_inc(gate_step.sem, 1)
                dve.wait_ge(gate_step.sem, gate_step.at(b, off, 1))
                nc.vector.tensor_tensor(g_prob[:], g_exp[:], g_inv[:].unsqueeze(2).to_broadcast([P, NT, E]),
                                        ALU.mult).then_inc(gate_step.sem, 1)
                dve.wait_ge(gate_step.sem, gate_step.at(b, off, 2))
                carry_wait()
                for t in range(NT):
                    last = nc.vector.max(g_top[:, t, :], g_prob[:, t, :])
                last.then_inc(gate_step.sem, 1)
                dve.wait_ge(gate_step.sem, gate_step.at(b, off, 3))
                nc.vector.tensor_tensor(g_two[:], g_top[:, :, 0:1], g_top[:, :, 1:2], ALU.add)
                for t in range(NT):
                    last = nc.vector.max_index(g_idx[:, t, :], g_top[:, t, :], g_prob[:, t, :])
                last.then_inc(gate_step.sem, 1)

            def gate_table(b, off):
                dve.wait_ge(gate_step.sem, gate_step.at(b, off, 4))
                nc.vector.tensor_copy(g_idf[:], g_idx[:])
                nc.vector.reciprocal(g_rtwo[:], g_two[:]).then_inc(gate_step.sem, 1)
                dve.wait_ge(gate_step.sem, gate_step.at(b, off, 5))
                nc.vector.tensor_tensor(g_val[:], g_top[:, :, 0:2], g_rtwo[:].to_broadcast([P, NT, 2]),
                                        ALU.mult).then_inc(gate_step.sem, 1)
                dve.wait_ge(gate_step.sem, gate_step.at(b, off, 6))
                for t in range(NT):
                    for i, one_hot in enumerate((g_first, g_second)):
                        last = nc.vector.tensor_scalar(one_hot[:, t, :], iota_sb[:], g_idf[:, t, i:i + 1],
                                                       g_val[:, t, i:i + 1], ALU.is_equal, ALU.mult)
                last.then_inc(gate_step.sem, 1)
                dve.wait_ge(gate_step.sem, gate_step.at(b, off, 7))
                nc.vector.tensor_tensor(gates[:], g_first[:], g_second[:], ALU.add).then_inc(gate_step.sem, 1)

            def row_maximum(b, s, h):
                dve.wait_ge(scored.sem, scored.at(b, 0, h + 1))
                ps = score_ps[s % 2]
                if h < H:
                    nc.vector.tensor_reduce(neg_max[:, h % STATS, :], ps[:].rearrange("p (t n) -> p t n", t=NT),
                                                         AX.X, ALU.max, negate=True).then_inc(max_ready.sem, 1)
                    return
                back = next(head_in(s - i) for i in (3, 6, 9) if head_in(s - i))
                dve.wait_ge(probs_turned.sem, probs_turned.at(b, back[0], back[1] + 1))
                if h == H:
                    dve.wait_ge(mask_ready.sem, mask_ready.at(b, 0, 1))
                for t in range(NT):
                    last = nc.vector.tensor_scalar(probs[:, s % P_BUFS, t, :], ps[:, t * T:(t + 1) * T],
                                                   mask_add[:, t:t + 1], None, ALU.subtract, ALU.min,
                                                   accum_out=neg_max[:, h % STATS, t:t + 1])
                last.then_inc(max_ready.sem, 1)

            def low_part(lo, ps, hi):
                return nc.vector.tensor_tensor(flat(lo), ps, flat(hi).bitcast(F32), ALU.subtract)

            def rope_products(ps):
                halves = ps.rearrange("p (t h n) -> p t h n", t=NT, h=2 * HG)
                for dst, table in ((rope_a, cos_sb), (rope_b, sin_sb)):
                    last = nc.vector.tensor_tensor(dst[:].rearrange("p t (h n) -> p t h n", h=2 * HG), halves,
                                                   table[:].unsqueeze(2).to_broadcast([P, NT, 2 * HG, HALF]),
                                                   ALU.mult)
                return last

            def unit(b, ps, kind, g, off):
                if kind == "QP":
                    dve.wait_ge(qk_projected.sem, qk_projected.at(b, off, 2 * g + 1))
                    dve.wait_ge(k_turned.sem, k_turned.at(b, off if g else off - 1, g if g else NG))
                    rope_products(ps).then_inc(rope_split.sem, 1)
                elif kind == "KP":
                    dve.wait_ge(qk_projected.sem, qk_projected.at(b, off, 2 * g + 2))
                    dve.wait_ge(q_turned.sem, q_turned.at(b, off, g + 1))
                    rope_products(ps).then_inc(rope_split.sem, 1)
                elif kind == "QT":
                    dve.wait_ge(q_hi_ready.sem, q_hi_ready.at(b, off, g + 1))
                    if g < NG:
                        last = nc.vector.scalar_tensor_tensor(flat(q_both[:, g % 2, 2:4, :]), ps, SCALE,
                                                              flat(q_both[:, g % 2, 0:2, :]).bitcast(F32),
                                                              ALU.mult, ALU.subtract)
                    else:
                        for i in range(2):
                            last = nc.vector.scalar_tensor_tensor(
                                head_half(q_both, g, i, 1 - i), half_of(ps, i), -SCALE,
                                head_half(q_both, g, i, i).bitcast(F32), ALU.mult, ALU.subtract)
                    last.then_inc(q_ready.sem, 1)
                elif kind == "KT":
                    dve.wait_ge(k_hi_ready.sem, k_hi_ready.at(b, off, g + 1))
                    if g < NG:
                        low_part(k_lo[:, g % 2, :, :], ps, k_both[:, g % 2, 0:2, :]).then_inc(k_ready.sem, 1)
                    else:
                        for i in range(2):
                            last = nc.vector.tensor_tensor(k_lo[i * HD:(i + 1) * HD, g % 2, :, :], half_of(ps, i),
                                                           head_half(k_both, g, i, i).bitcast(F32), ALU.subtract)
                        last.then_inc(k_ready.sem, 1)
                elif kind == "CT":
                    dve.wait_ge(ctx_hi_ready.sem, ctx_hi_ready.at(b, off, 1))
                    low_part(ct_lo[:], ps, ct_hi[:]).then_inc(ctx_ready.sem, 1)
                elif kind in ("L1", "L2"):
                    dve.wait_ge(xs_hi_ready.sem, xs_hi_ready.at(b, off, 1 if kind == "L1" else 2))
                    low_part(xs_lo[:], ps, xs_hi[:]).then_inc(xs_ready.sem, 1)
                elif kind == "L3":
                    dve.wait_ge(xf_hi_ready.sem, xf_hi_ready.at(b, off, 1))
                    low_part(xf_lo[:], ps, xf_hi[:]).then_inc(xf_ready.sem, 1)
                elif kind == "LG":
                    dve.wait_ge(logits_done.sem, logits_done.at(b, off, 1))
                    nc.vector.tensor_reduce(g_nmax[:], ps[:, 0:NT * E].rearrange("p (t n) -> p t n", t=NT),
                                            AX.X, ALU.max, negate=True).then_inc(gate_max.sem, 1)
                elif kind == "GT":
                    dve.wait_ge(gates_turned.sem, gates_turned.at(b, off, 1))
                    if exists(b, off + 1):
                        dve.wait_ge(roped.sem, roped.at(b, off + 1, 2 * NG))
                    nc.vector.tensor_copy(gatesT, ps[0:E, 0:T]).then_inc(gatesT_ready.sem, 1)
                elif kind == "BI":
                    dve.wait_ge(bias_done.sem, bias_done.at(b, off, 1))
                    dve.wait_ge(expert_added.sem, expert_added.at(b, off, 2 * E))
                    nc.vector.tensor_tensor(flat(x1[:]), ps, flat(x1[:]), ALU.add).then_inc(bias_added.sem, 1)
                elif kind == "EX":
                    j, t = divmod(g, NT)
                    dve.wait_ge(expert_done.sem, expert_done.at(b, off, g + 1))
                    if g < NT:
                        dve.wait_ge(gate_step.sem, gate_step.at(b, off, GATE_STEPS))
                    else:
                        dve.wait_ge(expert_added.sem, expert_added.at(b, off, 2 * (g - NT) + 2))
                    add_expert(ps, 2 * j, t).then_inc(expert_added.sem, 1)
                    dve.wait_ge(expert_added.sem, expert_added.at(b, off, 2 * g + 1))
                    add_expert(ps, 2 * j + 1, t).then_inc(expert_added.sem, 1)

            def add_expert(ps, e, t):
                i = e % 2
                return nc.vector.scalar_tensor_tensor(x1[:, t, :], ps[:, i * D:(i + 1) * D], gates[:, t, e:e + 1],
                                                      x1[:, t, :], ALU.mult, ALU.add)

            def residual(b, off, i):
                dve.wait_ge(wo_done.sem, wo_done.at(b, off, NG * (i + 1)))
                x = (x_in, x1)[i]
                if i == 0:
                    dve.wait_ge(x_loaded.sem, x_loaded.at(b, off, 1))
                nc.vector.tensor_tensor(x[:], wo_ps[:].rearrange("p (t n) -> p t n", t=NT),
                                                         x[:], ALU.add).then_inc(resid_done[i].sem, 1)
                dve.wait_ge(resid_done[i].sem, resid_done[i].at(b, off, 1))

            def oT_low(b, s):
                off, h, _ = meets_values(s)
                g = h // HG
                dve.wait_ge(oT_hi_ready.sem, oT_hi_ready.at(b, off, g + 1))
                nc.vector.tensor_tensor(flat(oT_lo[:]), oT_ps[:], flat(oT_hi[:]).bitcast(F32),
                                        ALU.subtract).then_inc(oT_ready.sem, 1)

            def body(b):
                for s in range(SLOTS):
                    here = head_in(s)
                    if here and exists(b, 0):
                        row_maximum(b, s, here[1])
                    for n, (kind, g, off, late) in enumerate(UNITS.get(s - 1, ())):
                        if exists(b, off) and late == LATE:
                            unit(b, unit_ps[unit_bank(s - 1, n) % 2][:], kind, g, off)
                    pair = meets_values(s)
                    group_ends = pair and pair[1] % HG == 2 and exists(b, pair[0])
                    if group_ends and s != AT["last values"][0]:
                        oT_low(b, s)
                    if s == AT["statistics 3"] and exists(b, -1):
                        layer_norm_stats(b, -1, 2, x1)
                    if s == AT["statistics 1"] and exists(b, 1):
                        dve.wait_ge(x_loaded.sem, x_loaded.at(b, 1, 1))
                        layer_norm_stats(b, 1, 0, x_in)
                    if s == AT["norm 3"] and exists(b, -1):
                        if exists(b, 0):
                            dve.wait_ge(xs_turned.sem, xs_turned.at(b, 0, 1))
                        else:
                            dve.wait_ge(xs_turned.sem, xs_turned.at(b, -1, 2))
                        layer_norm_apply(b, -1, 2, x1)
                    if s == AT["norm 1"] and exists(b, 1):
                        dve.wait_ge(xs_turned.sem, xs_turned.at(b, 0, 2))
                        layer_norm_apply(b, 1, 0, x_in)
                    for n, (kind, g, off, late) in enumerate(UNITS[s]):
                        if exists(b, off) and late != LATE:
                            unit(b, unit_ps[unit_bank(s, n) % 2][:], kind, g, off)
                        if [s, n] == AT["last values"] and group_ends:
                            oT_low(b, s)
                        if s == AT["statistics 2"][0] and n == AT["statistics 2"][1] and exists(b, 0):
                            residual(b, 0, 0)
                            layer_norm_stats(b, 0, 1, x_in)
                        if s == AT["norm 2"][0] and n == AT["norm 2"][1] and exists(b, 0):
                            dve.wait_ge(ctx_turned.sem, ctx_turned.at(b, 0, 1))
                            layer_norm_apply(b, 0, 1, x_in)
                    if s == AT["gate weights"] and exists(b, -1):
                        gate_weights(b, -1)
                    if s == AT["gate table"] and exists(b, -1):
                        gate_table(b, -1)
                    if s == AT["mask"] and exists(b, 0):
                        dve.wait_ge(mask_loaded.sem, mask_loaded.at(b, 0, 1))
                        nc.vector.tensor_scalar(mask_add[:], mask_i[:], -1.0, MASK_NEG,
                                                ALU.add, ALU.mult).then_inc(mask_ready.sem, 1)
                    if s == AT["residual 3"] and exists(b, -1):
                        residual(b, -1, 1)
                    if s == AT["x to x1"] and exists(b, 0):
                        dve.wait_ge(stored.sem, stored.at(b, -1, 1))
                        dve.wait_ge(bout_loaded.sem, bout_loaded.at(b, 0, 1))
                        nc.vector.tensor_tensor(x1[:], x_in[:], bout_sb.unsqueeze(1).to_broadcast([P, NT, D]),
                                                ALU.add).then_inc(x_moved.sem, 1)

            bodies(dve, body)

        @block.gpsimd
        def _(pool):
            nc.gpsimd.memset(neg_half[:], -0.5).then_inc(consts, 1)
            nc.gpsimd.memset(minus_one[:], -1.0).then_inc(consts, 1)
            nc.gpsimd.memset(ident[:], 0.0).then_inc(consts, 1)
            pool.wait_ge(consts, 3)
            nc.gpsimd.affine_select(out=ident[:], in_=ident[:], compare_op=ALU.not_equal, fill=1.0, base=0,
                                    pattern=[[-1, P]], channel_multiplier=1).then_inc(consts, 1)

            def standard_deviation(b, off, i):
                pool.wait_ge(ln_step[i].sem, ln_step[i].at(b, off, 3))
                nc.gpsimd.tensor_tensor(rstd[:, i, :], var_eps[:, i, :], neg_half[:],
                                        ALU.pow).then_inc(rstd_ready[i].sem, 1)

            def body(b):
                for s in range(SLOTS):
                    summed = head_in(s - 1)
                    if summed and exists(b, summed[0]):
                        off, h, hs = summed
                        inv = inv_sum[:, h % STATS, :]
                        pool.wait_ge(exp_done.sem, exp_done.at(b, off, h + 1))
                        nc.gpsimd.tensor_tensor(inv, row_sum[:, h % STATS, :], minus_one[:],
                                                ALU.pow).then_inc(inv_ready.sem, 1)
                        pool.wait_ge(inv_ready.sem, inv_ready.at(b, off, h + 1))
                        weights = probs[:, hs % P_BUFS, :, :]
                        nc.gpsimd.tensor_tensor(
                            weights, weights, inv.unsqueeze(2).to_broadcast([P, NT, T]),
                            ALU.mult).then_inc(probs_ready.sem, 1)
                    for kind, g, off, _ in UNITS.get(s - 1, ()):
                        if kind in ("QP", "KP") and exists(b, off):
                            k = 2 * g + (1 if kind == "QP" else 2)
                            pool.wait_ge(rope_split.sem, rope_split.at(b, off, k))
                            a = rope_a[:].rearrange("p t (h e n) -> p (t h) e n", h=HG, e=2)
                            r = rope_b[:].rearrange("p t (h e n) -> p (t h) e n", h=HG, e=2)
                            nc.gpsimd.tensor_tensor(a[:, :, 0, :], a[:, :, 0, :], r[:, :, 1, :],
                                                    ALU.subtract)
                            nc.gpsimd.tensor_tensor(a[:, :, 1, :], a[:, :, 1, :], r[:, :, 0, :],
                                                    ALU.add).then_inc(roped.sem, 1)
                    if s == AT["norm 2"][0] and exists(b, 0):
                        standard_deviation(b, 0, 1)
                    if s == AT["statistics 3"] and exists(b, -1):
                        standard_deviation(b, -1, 2)
                    if s == AT["statistics 1"] and exists(b, 1):
                        standard_deviation(b, 1, 0)

            bodies(pool, body)


def rotary_tables():
    pos = np.arange(T, dtype=np.float32)
    i = np.arange(HALF, dtype=np.float32)
    cos, sin = [], []
    for scale in (1.0, 4.0, 16.0):
        freqs = (np.float32(1.0) / np.float32(10000.0 * scale) ** (np.float32(2.0) * i / np.float32(HD)))
        ang = pos[:, None] * freqs[None, :].astype(np.float32)
        cos.append(np.cos(ang))
        sin.append(np.sin(ang))
    cos = np.mean(np.stack(cos), 0, dtype=np.float32)
    sin = np.mean(np.stack(sin), 0, dtype=np.float32)

    def by_partition(a):
        return np.ascontiguousarray(a.reshape(NT, P, HALF).transpose(1, 0, 2), np.float32)

    return by_partition(cos), by_partition(sin)


def kernel(**inputs):
    import concourse.bacc as bacc
    from concourse.bass_utils import run_bass_kernel_spmd as run

    def even_first(w):
        w = np.asarray(w)
        return np.ascontiguousarray(w.reshape(D, H, HALF, 2).transpose(0, 1, 3, 2).reshape(D, H * HD))

    cos, sin = rotary_tables()
    arrays = {
        "x": inputs["x"], "ctx": inputs["ctx_1024"],
        "mask": np.asarray(inputs["mask_BxS_ik0"]).reshape(B, NT, P).transpose(0, 2, 1),
        "sq": even_first(inputs["L0_attn_Wq"]), "sk": even_first(inputs["L0_attn_Wk"]),
        "sv": inputs["L0_attn_Wv"], "so": inputs["L0_attn_Wo"],
        "cq": inputs["L0_xattn_Wq"], "ckv": inputs["L0_xattn_Wkv"], "co": inputs["L0_xattn_Wout"],
        "bout": inputs["L0_xattn_bout"],
        "wg": inputs["L0_ffn_Wg"], "we": inputs["L0_ffn_We"], "be": inputs["L0_ffn_be"],
        "cos": cos, "sin": sin,
        "iota": np.tile(np.arange(E, dtype=np.float32), (P, 1)),
    }
    arrays = {k: np.ascontiguousarray(v) for k, v in arrays.items()}
    nc = bacc.Bacc("TRN2", target_bir_lowering=False, num_devices=1,
                   dynamic_dma_scratch_size=64)
    args = [nc.dram_tensor(f"dram_{k}", a.shape, mybir.dt.from_np(a.dtype), kind="ExternalInput").ap()
            for k, a in arrays.items()]
    out = nc.dram_tensor("layer_out", (B, T, D), F32, kind="ExternalOutput").ap()
    layer(nc, *args, out)
    r = run(nc, [{f"dram_{k}": a for k, a in arrays.items()}], core_ids=[0])
    return r.results[0]["layer_out"]
```
